# Optimizing a Trainium2 kernel written in Bass

```python
import numpy as np
import jax
import jax.numpy as jnp

def _softmax(x, axis=-1):
    return jax.nn.softmax(x, axis=axis)
def _gelu(x):
    return jax.nn.gelu(x, approximate=True)
def _silu(x):
    return jax.nn.silu(x)
def _sigmoid(x):
    return jax.nn.sigmoid(x)
def _layernorm(x, axis=-1, eps=1e-5):
    m = jnp.mean(x, axis=axis, keepdims=True)
    v = jnp.var(x, axis=axis, keepdims=True)
    return (x - m) / jnp.sqrt(v + eps)
def _scatter_add(tgt, idx, src, axis=0):
    return tgt.at[idx].add(src)
def _segment_sum(src, seg, n):
    return jax.ops.segment_sum(src, seg, n)

kernel_name = 'mk_conv_seq_d2_conv_nchw256_8c2a18'

def setup_inputs(seed: int = 0):
    np.random.seed(seed)
    _w = jnp.asarray
    def _rec_inputs():
        import jax
        import jax.numpy as jnp
        _gk = jax.random.key(seed)
        x = -0.0005153 + 1.001 * jax.random.normal(jax.random.fold_in(_gk, 1), (4, 256, 56, 56), jnp.float32)
        return x
    x = _rec_inputs()
    def _L0_conv_setup():
        import jax, jax.numpy as jnp
        import numpy as np
        from jax import lax
        EPS = 1e-05
        P, H_DIM = (32, 4)
        C = 256

        def _bn_nchw(x, g, b):
            m = jnp.mean(x, axis=(0, 2, 3), keepdims=True)
            v = jnp.var(x, axis=(0, 2, 3), keepdims=True)
            return (x - m) * (g[None, :, None, None] / jnp.sqrt(v + EPS)) + b[None, :, None, None]

        def _bn_paths(x, g, b):
            m = jnp.mean(x, axis=(0, 3, 4), keepdims=True)
            v = jnp.var(x, axis=(0, 3, 4), keepdims=True)
            return (x - m) * (g[None, :, :, None, None] / jnp.sqrt(v + EPS)) + b[None, :, :, None, None]
        key = jax.random.key(seed)
        ks = jax.random.split(key, 8)
        B, H, W = (4, 56, 56)
        x = jax.random.normal(ks[0], (B, C, H, W), dtype=jnp.float32)
        w1 = jax.random.normal(ks[1], (P * H_DIM, C), dtype=jnp.float32) * 0.01
        b1 = jax.random.normal(ks[2], (P * H_DIM,), dtype=jnp.float32) * 0.01
        w2 = jax.random.normal(ks[3], (P * H_DIM, H_DIM, 3, 3), dtype=jnp.float32) * 0.01
        b2 = jax.random.normal(ks[4], (P * H_DIM,), dtype=jnp.float32) * 0.01
        w3 = jax.random.normal(ks[5], (P, C, H_DIM), dtype=jnp.float32) * 0.01
        b3 = jax.random.normal(ks[6], (P, C), dtype=jnp.float32) * 0.01
        g1 = jnp.ones((P * H_DIM,), jnp.float32)
        be1 = jnp.zeros((P * H_DIM,), jnp.float32)
        g2 = jnp.ones((P * H_DIM,), jnp.float32)
        be2 = jnp.zeros((P * H_DIM,), jnp.float32)
        g3 = jnp.ones((P, C), jnp.float32)
        be3 = jnp.zeros((P, C), jnp.float32)
        g4 = jnp.ones((C,), jnp.float32)
        be4 = jnp.zeros((C,), jnp.float32)
        return {'x': x, 'w1': w1, 'b1': b1, 'g1': g1, 'be1': be1, 'w2': w2, 'b2': b2, 'g2': g2, 'be2': be2, 'w3': w3, 'b3': b3, 'g3': g3, 'be3': be3, 'g4': g4, 'be4': be4}
    _L0_conv_all = _L0_conv_setup()
    _L0_conv_in = {k: v for k, v in _L0_conv_all.items() if k in ('w1', 'b1', 'g1', 'be1', 'w2', 'b2', 'g2', 'be2', 'w3', 'b3', 'g3', 'be3', 'g4', 'be4', )}
    del _L0_conv_all

    def _L1_conv_setup():
        import jax, jax.numpy as jnp
        import numpy as np
        key = jax.random.key(seed)
        kx, kq, kk, kv = jax.random.split(key, 4)
        B, C, H, W = (4, 256, 64, 64)
        scale = 1.0 / np.sqrt(C)
        return {'x': jax.random.normal(kx, (B, C, H, W), dtype=jnp.float32), 'Wq': jax.random.normal(kq, (C, C), dtype=jnp.float32) * scale, 'Wk': jax.random.normal(kk, (C, C), dtype=jnp.float32) * scale, 'Wv': jax.random.normal(kv, (C, C), dtype=jnp.float32) * scale, 'gamma': jnp.ones((1,), dtype=jnp.float32) * 0.1}
    _L1_conv_all = _L1_conv_setup()
    _L1_conv_in = {k: v for k, v in _L1_conv_all.items() if k in ('Wq', 'Wk', 'Wv', 'gamma', )}
    del _L1_conv_all

    return {
        "x": x,
        "L0_conv_w1": _L0_conv_in["w1"],
        "L0_conv_b1": _L0_conv_in["b1"],
        "L0_conv_g1": _L0_conv_in["g1"],
        "L0_conv_be1": _L0_conv_in["be1"],
        "L0_conv_w2": _L0_conv_in["w2"],
        "L0_conv_b2": _L0_conv_in["b2"],
        "L0_conv_g2": _L0_conv_in["g2"],
        "L0_conv_be2": _L0_conv_in["be2"],
        "L0_conv_w3": _L0_conv_in["w3"],
        "L0_conv_b3": _L0_conv_in["b3"],
        "L0_conv_g3": _L0_conv_in["g3"],
        "L0_conv_be3": _L0_conv_in["be3"],
        "L0_conv_g4": _L0_conv_in["g4"],
        "L0_conv_be4": _L0_conv_in["be4"],
        "L1_conv_Wq": _L1_conv_in["Wq"],
        "L1_conv_Wk": _L1_conv_in["Wk"],
        "L1_conv_Wv": _L1_conv_in["Wv"],
        "L1_conv_gamma": _L1_conv_in["gamma"],
    }

def reference(x, L0_conv_w1, L0_conv_b1, L0_conv_g1, L0_conv_be1, L0_conv_w2, L0_conv_b2, L0_conv_g2, L0_conv_be2, L0_conv_w3, L0_conv_b3, L0_conv_g3, L0_conv_be3, L0_conv_g4, L0_conv_be4, L1_conv_Wq, L1_conv_Wk, L1_conv_Wv, L1_conv_gamma):
    import jax
    import jax.numpy as jnp
    def _L0_conv_ref(x, w1, b1, g1, be1, w2, b2, g2, be2, w3, b3, g3, be3, g4, be4):
        import jax, jax.numpy as jnp
        import numpy as np
        from jax import lax
        EPS = 1e-05
        P, H_DIM = (32, 4)
        C = 256

        def _bn_nchw(x, g, b):
            m = jnp.mean(x, axis=(0, 2, 3), keepdims=True)
            v = jnp.var(x, axis=(0, 2, 3), keepdims=True)
            return (x - m) * (g[None, :, None, None] / jnp.sqrt(v + EPS)) + b[None, :, None, None]

        def _bn_paths(x, g, b):
            m = jnp.mean(x, axis=(0, 3, 4), keepdims=True)
            v = jnp.var(x, axis=(0, 3, 4), keepdims=True)
            return (x - m) * (g[None, :, :, None, None] / jnp.sqrt(v + EPS)) + b[None, :, :, None, None]
        y = jnp.einsum('bchw,kc->bkhw', x, w1) + b1[None, :, None, None]
        y = jax.nn.relu(_bn_nchw(y, g1, be1))
        y = lax.conv_general_dilated(y, w2, window_strides=(1, 1), padding=[(1, 1), (1, 1)], feature_group_count=P, dimension_numbers=('NCHW', 'OIHW', 'NCHW'))
        y = y + b2[None, :, None, None]
        y = jax.nn.relu(_bn_nchw(y, g2, be2))
        B, _, Hh, Ww = y.shape
        y = y.reshape(B, P, H_DIM, Hh, Ww)
        y = jnp.einsum('bphxy,pch->bpcxy', y, w3) + b3[None, :, :, None, None]
        y = jax.nn.relu(_bn_paths(y, g3, be3))
        s = jnp.sum(y, axis=1) + x
        return _bn_nchw(s, g4, be4)

    def _L1_conv_ref(x, Wq, Wk, Wv, gamma):
        import jax, jax.numpy as jnp
        import numpy as np
        B, C, H, W = x.shape
        N = H * W
        xt = x.reshape(B, C, N)
        q = jnp.einsum('oc,bcn->bon', Wq, xt)
        k = jnp.einsum('oc,bcn->bon', Wk, xt)
        v = jnp.einsum('oc,bcn->bon', Wv, xt)
        energy = jnp.einsum('bon,bom->bnm', q, k)
        attn = jax.nn.softmax(energy, axis=-1)
        out = jnp.einsum('bcm,bnm->bcn', v, attn).reshape(B, C, H, W)
        return gamma * out + x

    def _gn(v, G=32, eps=1e-5):
        B_, C_, H_, W_ = v.shape
        g = v.reshape(B_, G, C_ // G, H_, W_)
        m = jnp.mean(g, axis=(2, 3, 4), keepdims=True)
        s = jnp.var(g, axis=(2, 3, 4), keepdims=True)
        return ((g - m) / jnp.sqrt(s + eps)).reshape(v.shape)

    def _ln_c(v, eps=1e-6):
        m = jnp.mean(v, axis=1, keepdims=True)
        s = jnp.var(v, axis=1, keepdims=True)
        return (v - m) / jnp.sqrt(s + eps)

    def _ln_t(v, eps=1e-5):
        m = jnp.mean(v, axis=-1, keepdims=True)
        s = jnp.var(v, axis=-1, keepdims=True)
        return (v - m) / jnp.sqrt(s + eps)

    def _to_tokens(v):
        B_, C_, H_, W_ = v.shape
        return v.reshape(B_, C_, H_ * W_).transpose(0, 2, 1)
    def _from_tokens(t, like):
        B_, C_, H_, W_ = like.shape
        return t.transpose(0, 2, 1).reshape(B_, C_, H_, W_)

    x = _L0_conv_ref(x, L0_conv_w1, L0_conv_b1, L0_conv_g1, L0_conv_be1, L0_conv_w2, L0_conv_b2, L0_conv_g2, L0_conv_be2, L0_conv_w3, L0_conv_b3, L0_conv_g3, L0_conv_be3, L0_conv_g4, L0_conv_be4)
    x = _L1_conv_ref(x, L1_conv_Wq, L1_conv_Wk, L1_conv_Wv, L1_conv_gamma)
    return x


_drawn_inputs = setup_inputs


def setup_inputs(seed=0):
    import zlib

    import numpy as np

    out = dict(_drawn_inputs(seed))
    spreads = {'L0_conv_g1': (1.0, 0.2),
     'L0_conv_be1': (0.0, 0.1),
     'L0_conv_g2': (1.0, 0.2),
     'L0_conv_be2': (0.0, 0.1),
     'L0_conv_g3': (1.0, 0.2),
     'L0_conv_be3': (0.0, 0.1),
     'L0_conv_g4': (1.0, 0.2),
     'L0_conv_be4': (0.0, 0.1)}
    factors = {}
    for name, (base, spread) in spreads.items():
        noise = np.random.default_rng([zlib.crc32(name.encode()), seed]).standard_normal(out[name].shape)
        drawn = base * np.exp(spread * noise) if base else spread * noise
        out[name] = jnp.asarray(drawn.astype(out[name].dtype))
    for name, factor in factors.items():
        out[name] = (out[name] * factor).astype(out[name].dtype)
    return out
```

```python
import concourse.bass as bass
from concourse import mybir

F32 = mybir.dt.float32
F32R = mybir.dt.float32r
ALU = mybir.AluOpType
ACT = mybir.ActivationFunctionType
AX = mybir.AxisListType

PART = 128
BATCH, CIN, IMG = 4, 256, 56
HALVES = CIN // PART
PIX = IMG * IMG
PATHS, HDIM = 32, 4
ROWS = 8
CHUNK = ROWS * IMG
NCH = PIX // CHUNK
NALL = BATCH * NCH
TOTAL = BATCH * PIX
PADW = IMG + 2
TAPS = 9
EPS = 1e-5
BN6 = 6

BLOCKS = 4
BPATHS = PATHS // BLOCKS
BROWS = PART // BLOCKS
KROWS = 3 * BROWS + 2
PAIRRING = 4
BY_ACT = (2, 5, 8, 11, 14, 17, 20, 23, 26, 29)
N_ACT = len(BY_ACT)
N_DVE = PATHS - N_ACT

MT = [PART] * 23 + [96, 96]
NMT = len(MT)
MOFF = [sum(MT[:i]) for i in range(NMT)]
QSUB = CHUNK // 4
SRING = 4
PRING = 3
LAG = 3
PIECE = 2 * CHUNK
PIECES = [PIECE, PIECE, PIECE, CHUNK]
UNITS = sum(2 * (w // CHUNK) for w in PIECES) + NMT
USLACK = 3


def conv_attention_kernel(nc, x, w1, b1, g1, be1, w2, b2, g2, be2, w3, b3, g3, be3, g4, be4,
                          wq, wk, wv, gamma, out):
    x_v = x.rearrange("b (k p) h w -> b p k (h w)", p=PART)
    s_spill = nc.dram_tensor("s_spill", (PART, HALVES, TOTAL), F32, kind="Internal").ap()

    base = (nc.sbuf_base + 31) // 32 * 32
    cursor = [base]

    def place(name, shape, dtype=F32, at=None):
        size = 4
        for n in shape[1:]:
            size *= n
        offset = cursor[0] if at is None else at
        if at is None:
            cursor[0] += (size + 31) // 32 * 32
        return nc.alloc_sbuf_tensor_at(name, list(shape), dtype, offset=offset)

    ident = place("ident", [PART, PART])
    ones = place("ones", [PART, PART])
    groups = place("groups", [PART, PART])
    at_hi = place("at_hi", [PART, HALVES, CIN], F32R)
    at_lo = place("at_lo", [PART, HALVES, CIN], F32R)
    wv_hi = place("wv_hi", [PART, HALVES, CIN], F32R)
    wv_lo = place("wv_lo", [PART, HALVES, CIN], F32R)
    vec = place("vec", [PART, 64])
    col = {}

    def c1(name, n=1):
        if name not in col:
            col[name] = (sum(w for _, w in col.values()), n)
            assert sum(w for _, w in col.values()) <= 64
        at, w = col[name]
        return vec[:, at:at + w]

    mean_var = place("mean_var", [PART, HALVES, 2])
    gamma_row = place("gamma_row", [1, 1])
    l0_base = cursor[0]

    y_raw = place("y_raw", [PART, BATCH, PIX])
    pad_at = [cursor[0], cursor[0] + BATCH * PADW * PADW * 4]
    y1_hi = place("y1_hi", [PART, BATCH, PADW, PADW], F32R)
    y1_lo = place("y1_lo", [PART, BATCH, PADW, PADW], F32R)
    y2_hi = place("y2_hi", [PART, BATCH, PIX], F32R, at=pad_at[0])
    y2_lo = place("y2_lo", [PART, BATCH, PIX], F32R, at=pad_at[1])
    spare = [p + TOTAL * 4 for p in pad_at]
    w1_t = place("w1_t", [PART, HALVES, PART])
    w3_t = place("w3_t", [PART, CIN])
    g3_b = place("g3_b", [PART, CIN])
    be3_b = place("be3_b", [PART, CIN])
    b3_b = place("b3_b", [PART, CIN])
    stats = place("stats", [PART, HALVES, NALL, BN6])
    tmp_at = cursor[0]
    tmp = [place(f"tmp{i}", [PART, CIN]) for i in range(6)]
    ws_hi = place("ws_hi", [PART, CIN], F32R)
    ws_lo = place("ws_lo", [PART, CIN], F32R)
    bias_hi = place("bias_hi", [PART, CIN], F32R)
    bias_lo = place("bias_lo", [PART, CIN], F32R)
    ring_at = cursor[0]
    x_ring = place("x_ring", [PART, BATCH, HALVES, CHUNK])
    y1_f = place("y1_f", [PART, BATCH, CHUNK], at=ring_at)
    y2_c = place("y2_c", [PART, BATCH, CHUNK], at=ring_at)
    y2_t = place("y2_t", [QSUB, 2, 4 * PART], at=ring_at + BATCH * CHUNK * 4)
    taps_at = cursor[0]
    taps_f = place("taps_f", [PART, TAPS, PART])
    taps_hi = place("taps_hi", [PART, TAPS, PART], F32R)
    taps_lo = place("taps_lo", [PART, TAPS, PART], F32R)
    l0_end = cursor[0]
    w1_n = place("w1_n", [PART, CIN], at=pad_at[1])
    w2_n = place("w2_n", [PART, HDIM * TAPS], at=pad_at[1] + 1024)
    w3_n = place("w3_n", [PART, HALVES, PATHS * HDIM], at=pad_at[1] + 2048)
    wq_n = place("wq_n", [PART, HALVES, CIN], at=pad_at[1] + 4096)
    wk_n = place("wk_n", [PART, HALVES, CIN], at=pad_at[1] + 6144)
    wv_n = place("wv_n", [PART, HALVES, CIN], at=pad_at[1] + 8192)
    wide = HALVES * CHUNK * 4
    path_w = place("path_w", [KROWS, PATHS, CIN], F32R, at=l0_base)
    staged = [[place(f"staged{i}_{g}", [KROWS, CHUNK], F32R,
                     at=l0_base + PATHS * CIN * 4 + (i * BLOCKS + g) * CHUNK * 4)
               for g in range(BLOCKS)] for i in range(2)]
    act_out = [place(f"act_out{i}", [PART, HALVES, CHUNK], at=ring_at + i * wide) for i in range(2)]
    pool_sum = [place(f"pool_sum{i}", [PART, HALVES, CHUNK], at=ring_at + (2 + i) * wide)
                for i in range(2)]
    dve_sum = [place(f"dve_sum{i}", [PART, HALVES, CHUNK], at=taps_at + i * wide)
               for i in range(2)]
    s_out = [place("s_out0", [PART, HALVES, CHUNK], at=taps_at + 2 * wide),
             place("s_out1", [PART, HALVES, CHUNK], at=tmp_at)]
    x_again = [place(f"x_again{i}", [PART, HALVES, CHUNK], at=spare[i]) for i in range(2)]

    cursor[0] = l0_base
    t_hi = place("t_hi", [PART, HALVES, PIX], F32R)
    t_lo = place("t_lo", [PART, HALVES, PIX], F32R)
    v_hi = place("v_hi", [PART, NMT, CIN], F32R)
    v_lo = place("v_lo", [PART, NMT, CIN], F32R)
    scores_at = cursor[0]
    scores = place("scores", [PART, NMT, CHUNK])
    p_f = place("p_f", [PART, PRING, CHUNK])
    p_hi = place("p_hi", [PART, PRING, CHUNK], F32R)
    p_lo = place("p_lo", [PART, PRING, CHUNK], F32R)
    xq_hi = place("xq_hi", [PART, 2, HALVES, CHUNK], F32R)
    xq_lo = place("xq_lo", [PART, 2, HALVES, CHUNK], F32R)
    xq_f = place("xq_f", [PART, 2, HALVES, CHUNK])
    x_res = place("x_res", [PART, HALVES, CHUNK])
    row_max = place("row_max", [PART, CHUNK])
    max_b = place("max_b", [PART, CHUNK])
    p_sum = place("p_sum", [PART, CHUNK])
    o_buf = place("o_buf", [PART, HALVES, CHUNK])
    diag = place("diag", [QSUB, 4, QSUB])
    max_q = place("max_q", [QSUB, 4])
    l1_end = cursor[0]
    recip_b = max_b
    assert max(l0_end, l1_end) <= nc.sbuf_usable_end, (l0_end, l1_end, nc.sbuf_usable_end)
    xp_f = [place(f"xp_f{i}", [PART, HALVES, PIECE], at=scores_at + i * 3 * HALVES * PIECE * 4)
            for i in range(2)]
    xp_hi = [place(f"xp_hi{i}", [PART, HALVES, PIECE], F32R,
                   at=scores_at + (i * 3 + 1) * HALVES * PIECE * 4) for i in range(2)]
    xp_lo = [place(f"xp_lo{i}", [PART, HALVES, PIECE], F32R,
                   at=scores_at + (i * 3 + 2) * HALVES * PIECE * 4) for i in range(2)]

    ps = nc.alloc_psum_tensor("ps", [PART, 8, 512], F32)
    BANK_O, BANK_MAX, BANK_SUM = 4, 6, 7

    def sem(name):
        return nc.alloc_semaphore(name)

    zero = tmp[5][:, 0:PART]

    def y2t_slot(b):
        return y2_t[:, b % 2]

    def bank(n, width, parts):
        return ps[:, n, 0:width].rearrange("p (k n) -> p k n", k=parts)

    setup_parts = [(3, bank(5, 2 * CIN, 2), at_hi[:, :, :], at_lo[:, :, :]),
                   (4, bank(6, 2 * CIN, 2), wv_hi[:, :, :], wv_lo[:, :, :])]
    for n, t in enumerate(range(0, TAPS, 4)):
        w = min(4, TAPS - t)
        setup_parts.append((6 + n, bank(2 + n, w * PART, w), taps_hi[:, t:t + w],
                            taps_lo[:, t:t + w]))

    def proj_units():
        units = []
        for q, w in enumerate(PIECES):
            xh, xl = xp_hi[q % 2], xp_lo[q % 2]
            for c in range(w // CHUNK):
                px = slice(c * CHUNK, (c + 1) * CHUNK)
                for h in range(HALVES):
                    o, pairs = slice(h * PART, (h + 1) * PART), []
                    for k in range(HALVES):
                        pairs += [(at_hi[:, k, o], xh[:, k, px]), (at_hi[:, k, o], xl[:, k, px]),
                                  (at_lo[:, k, o], xh[:, k, px])]
                    dst = slice(q * PIECE + c * CHUNK, q * PIECE + (c + 1) * CHUNK)
                    units.append((q, pairs, t_hi[:, h, dst], t_lo[:, h, dst]))
            for i in range(NMT):
                if not q * PIECE <= MOFF[i] < q * PIECE + w:
                    continue
                m, pairs = MT[i], []
                px = slice(MOFF[i] - q * PIECE, MOFF[i] - q * PIECE + m)
                for k in range(HALVES):
                    pairs += [(xh[:, k, px], wv_hi[:, k]), (xh[:, k, px], wv_lo[:, k]),
                              (xl[:, k, px], wv_hi[:, k])]
                units.append((q, pairs, v_hi[0:m, i], v_lo[0:m, i]))
        assert len(units) == UNITS
        return units

    def ps_unit(at, unit):
        rows, width = unit[2].shape[0], unit[2].shape[-1]
        return ps[0:rows, at % SRING, 0:width]

    taps_made = sem("taps_made")
    zero_made = sem("zero_made")
    gram_free = sem("gram_free")
    consts_made = sem("consts_made")
    weights_loaded = sem("weights_loaded")
    setup_mm = sem("setup_mm")
    setup_hi = sem("setup_hi")
    setup_done = sem("setup_done")
    pad_zeroed = sem("pad_zeroed")
    dve_step = sem("dve_step")
    sd_ready = sem("sd_ready")
    var_ready = sem("var_ready")
    x_loaded = [sem(f"x_loaded{b}") for b in range(BATCH)]
    conv1_done = sem("conv1_done")
    y1_stored = sem("y1_stored")
    y1_stats = sem("y1_stats")
    bn1_ready = sem("bn1_ready")
    y1_act = sem("y1_act")
    y1_hi_done = sem("y1_hi_done")
    y1_split = sem("y1_split")
    conv2_done = sem("conv2_done")
    y2_stored = sem("y2_stored")
    y2_stats = sem("y2_stats")
    bn2_ready = sem("bn2_ready")
    y2_act = sem("y2_act")
    y2_mean = sem("y2_mean")
    y2_hi_done = sem("y2_hi_done")
    y2_split = sem("y2_split")
    y2_centred = sem("y2_centred")
    y2_turned = sem("y2_turned")
    y2_t_ready = sem("y2_t_ready")
    gram_done = sem("gram_done")
    cov_ready = sem("cov_ready")
    wcov_done = sem("wcov_done")
    path_w_ready = sem("path_w_ready")
    path_rows_copied = sem("path_rows_copied")
    bias_ready = sem("bias_ready")
    ones_rows = sem("ones_rows")
    staged_in = [sem(f"staged_in{i}") for i in range(2)]
    x_again_in = [sem(f"x_again_in{i}") for i in range(2)]
    z_done = sem("z_done")
    dve_read = sem("dve_read")
    act_read = sem("act_read")
    pool_added = sem("pool_added")
    dve_added = sem("dve_added")
    s_ready = sem("s_ready")
    s_stats = sem("s_stats")
    s_stored = [sem(f"s_stored{i}") for i in range(2)]
    bn4_ready = sem("bn4_ready")
    xp_loaded = [sem(f"xp_loaded{i}") for i in range(2)]
    xp_normed = sem("xp_normed")
    xp_hi_done = sem("xp_hi_done")
    xp_split = sem("xp_split")
    proj_done = sem("proj_done")
    proj_hi = sem("proj_hi")
    proj_lo = sem("proj_lo")
    xq_loaded = sem("xq_loaded")
    xq_step = sem("xq_step")
    xq_split = sem("xq_split")
    xr_loaded = sem("xr_loaded")
    xr_normed = sem("xr_normed")
    qk_done = sem("qk_done")
    s_evac = sem("s_evac")
    max_done = sem("max_done")
    max_turned = sem("max_turned")
    maxq_done = sem("maxq_done")
    diag_done = sem("diag_done")
    maxb_done = sem("maxb_done")
    maxb_ready = sem("maxb_ready")
    sub_done = sem("sub_done")
    exp_done = sem("exp_done")
    hi_done = sem("hi_done")
    lo_done = sem("lo_done")
    sum_added = sem("sum_added")
    pv_done = sem("pv_done")
    l_done = sem("l_done")
    linv_done = sem("linv_done")
    o_read = sem("o_read")
    out_added = sem("out_added")
    out_stored = sem("out_stored")

    N_WEIGHTS = 30

    def chunk_of(b, j):
        return y_raw[:, b, bass.ds(j * CHUNK, CHUNK)]

    def padded(t, b, row, rows, left):
        return t[:, b, bass.ds(row, rows), left:left + IMG]

    def xq_slot(t, i):
        return t[:, bass.ds(i, 1)].rearrange("p o k n -> p (o k) n")

    def out_at(b, j):
        return out.rearrange("b (k p) h w -> p k b (h w)", p=PART)[
            :, :, bass.ds(b, 1), bass.ds(j * CHUNK, CHUNK)].rearrange("p k o n -> p k (o n)")

    with nc.Block() as block:

        @block.sync
        def _(sp):
            def weight(dst, src):
                sp.dma_start(dst, src).then_inc(weights_loaded, 16)

            def column(v):
                return v.rearrange("(p o) -> p o", o=1)

            weight(w1_n[:, :], w1)
            weight(w2_n[:, :], w2.rearrange("k i a b -> k (i a b)"))
            for k in range(HALVES):
                weight(w3_n[:, k, :].rearrange("p (a h) -> p a h", h=HDIM),
                       w3[:, k * PART:(k + 1) * PART, :].rearrange("a c h -> c a h"))
            weight(c1("b1"), column(b1))
            weight(c1("b2"), column(b2))
            weight(c1("g1"), column(g1))
            weight(c1("be1"), column(be1))
            for b in range(BATCH):
                sp.dma_start(x_ring[:, b], x_v[b][:, :, 0:CHUNK]).then_inc(x_loaded[b], 16)
            weight(c1("g2"), column(g2))
            weight(c1("be2"), column(be2))
            for k in range(HALVES):
                half = slice(k * PART, (k + 1) * PART)
                weight(c1("g4", 2)[:, k:k + 1], column(g4[half]))
                weight(c1("be4", 2)[:, k:k + 1], column(be4[half]))
            for t, w in ((wq_n, wq), (wk_n, wk), (wv_n, wv)):
                weight(t[:, :, :], w.rearrange("(k p) c -> p k c", p=PART))
            for t, w in ((g3_b, g3), (be3_b, be3), (b3_b, b3)):
                for h in range(HDIM):
                    weight(t[h:PART:HDIM, :], w)
            weight(gamma_row[:, :], gamma.rearrange("(p o) -> p o", o=1))
            with sp.Fori(1, NCH) as j:
                for b in range(BATCH):
                    sp.wait_ge(conv1_done, j * BATCH + b - BATCH + 1)
                    sp.dma_start(x_ring[:, b], x_v[b][:, :, bass.ds(j * CHUNK, CHUNK)])\
                      .then_inc(x_loaded[b], 16)

            sp.wait_ge(path_w_ready, 1)
            sp.dma_start(path_w[BROWS:2 * BROWS].bitcast(F32), path_w[0:BROWS].bitcast(F32))\
             .then_inc(path_rows_copied, 16)
            sp.wait_ge(bias_ready, 1)
            for r, t in ((0, bias_hi), (1, bias_lo)):
                row = 3 * BROWS + r
                sp.dma_start(path_w[row:row + 1, :, :].bitcast(F32), t[0:PART:HDIM, :].bitcast(F32))\
                  .then_inc(path_rows_copied, 16)

            def load_chunk(j, b):
                i = b % 2
                for g in range(BLOCKS):
                    rows = slice(g * BROWS, (g + 1) * BROWS)
                    for r, t in ((0, y2_hi), (1, y2_lo), (2, y2_hi)):
                        sp.dma_start(staged[i][g][r * BROWS:(r + 1) * BROWS, :].bitcast(F32),
                                     t[rows, b, bass.ds(j * CHUNK, CHUNK)].bitcast(F32))\
                          .then_inc(staged_in[i], 16)
                sp.dma_start(x_again[i][:, :, :], x_v[b][:, :, bass.ds(j * CHUNK, CHUNK)])\
                  .then_inc(x_again_in[i], 16)

            sp.wait_ge(y2_split, NALL)
            sp.wait_ge(gram_done, 1)
            sp.wait_ge(ones_rows, 2 * BLOCKS)
            load_chunk(0, 0)
            load_chunk(0, 1)

            def finish(j, b, following):
                sp.wait_ge(s_ready, 2 + j * BATCH + b + 1)
                sp.dma_start(s_spill[:, :, bass.ds(b * PIX + j * CHUNK, CHUNK)],
                             s_out[b % 2][:, :, :]).then_inc(s_stored[b % 2], 16)
                if following:
                    load_chunk(*following)

            with sp.Fori(0, NCH - 1) as j:
                for b in range(BATCH):
                    finish(j, b, (j, b + 2) if b < 2 else (j + 1, b - 2))
            for b in range(BATCH):
                finish(NCH - 1, b, (NCH - 1, b + 2) if b < 2 else None)

            for i in range(2):
                sp.wait_ge(s_stored[i], 16 * NALL // 2)
            sp.wait_ge(bn4_ready, 1)

            for g in range(2):
                sp.wait_ge(xq_loaded, g * 16)
                sp.dma_start(xq_f[:, g], s_spill[:, :, g * CHUNK:(g + 1) * CHUNK])\
                  .then_inc(xq_loaded, 16)

            def stage(g):
                sp.wait_ge(xq_split, g + 1)
                sp.wait_ge(xq_loaded, g * 16 + 32)
                n = (g + 2) % NALL
                sp.dma_start(xq_slot(xq_f, g % 2),
                             s_spill[:, :, bass.ds(n * CHUNK, CHUNK)]).then_inc(xq_loaded, 16)
                sp.wait_ge(out_added, g)
                sp.dma_start(x_res[:, :, :], s_spill[:, :, bass.ds(g * CHUNK, CHUNK)])\
                  .then_inc(xr_loaded, 16)

            with sp.Fori(0, BATCH) as b:
                sp.wait_ge(sub_done, b * NCH * NMT)
                for q, w in enumerate(PIECES):
                    if q >= 2:
                        sp.wait_ge(xp_split, b * len(PIECES) + q - 1)
                    sp.dma_start(xp_f[q % 2][:, :, 0:w],
                                 s_spill[:, :, bass.ds(b * PIX + q * PIECE, w)])\
                      .then_inc(xp_loaded[q % 2], 16)
                with sp.Fori(0, NCH) as j:
                    g = b * NCH + j
                    stage(g)
                    sp.wait_ge(out_added, g + 1)
                    sp.dma_start(out_at(b, j), o_buf[:, :, :]).then_inc(out_stored, 16)
            sp.wait_ge(out_stored, 16 * NALL)
            sp.wait_ge(xq_loaded, 16 * (NALL + 2))

        @block.gpsimd
        def _(pool):
            pool.memset(ident[:, :], 0.0).then_inc(consts_made, 1)
            pool.memset(ones[:, :], 1.0).then_inc(consts_made, 1)
            pool.memset(groups[:, :], 1.0).then_inc(consts_made, 1)
            pool.wait_ge(consts_made, 3)
            pool.affine_select(out=ident[:, :], in_=ident[:, :], compare_op=ALU.not_equal, fill=1.0,
                               base=0, pattern=[[-1, PART]], channel_multiplier=1)\
                .then_inc(consts_made, 1)
            grid = groups[:, :].rearrange("p (a h) -> p a h", h=HDIM)
            pool.affine_select(out=grid, in_=grid, compare_op=ALU.is_ge, fill=0.0, base=0,
                               pattern=[[-HDIM, PATHS], [0, HDIM]], channel_multiplier=1)\
                .then_inc(consts_made, 1)
            pool.wait_ge(consts_made, 5)
            pool.affine_select(out=grid, in_=grid, compare_op=ALU.is_ge, fill=0.0, base=HDIM - 1,
                               pattern=[[HDIM, PATHS], [0, HDIM]], channel_multiplier=-1)\
                .then_inc(consts_made, 1)
            pool.memset(y1_hi[:, :, :, :].bitcast(F32), 0.0).then_inc(pad_zeroed, 1)
            pool.wait_ge(setup_done, 1)
            pool.memset(y1_lo[:, :, :, :].bitcast(F32), 0.0).then_inc(pad_zeroed, 1)

            pool.wait_ge(gram_done, 1)
            n = 0
            for i in range(2):
                for g in range(BLOCKS):
                    pool.memset(staged[i][g][3 * BROWS:KROWS, :].bitcast(F32), 1.0).then_inc(ones_rows, 1)

            with pool.Fori(0, NCH) as j:
                for b in range(BATCH):
                    i, n = b % 2, j * BATCH + b
                    pool.wait_ge(x_again_in[i], (j * 2 + b // 2 + 1) * 16)
                    pool.wait_ge(s_ready, n + 1)
                    for k in range(N_ACT):
                        pool.wait_ge(act_read, (n + 1) * N_ACT + k + 1)
                        if k:
                            pool.wait_ge(pool_added, n * N_ACT + k)
                        pool.tensor_tensor(pool_sum[i][:, :, :], act_out[k % 2][:, :, :],
                                           (x_again[i] if k == 0 else pool_sum[i])[:, :, :],
                                           ALU.add).then_inc(pool_added, 1)

            with pool.Fori(0, NALL) as g:
                pool.wait_ge(l_done, g)
                for i in range(1, NMT):
                    m = MT[i]
                    pool.wait_ge(exp_done, g * NMT + i + 1)
                    if i > 1:
                        pool.wait_ge(sum_added, g * (NMT - 1) + i - 1)
                    pool.tensor_tensor(p_sum[0:m, :], p_f[0:m, i % PRING],
                                       (p_f[0:m, 0] if i == 1 else p_sum[0:m, :]), ALU.add)\
                        .then_inc(sum_added, 1)
                pool.wait_ge(o_read, (g + 1) * HALVES)
                pool.wait_ge(xr_normed, g * HALVES + HALVES)
                pool.tensor_tensor(o_buf[:, :, :], o_buf[:, :, :], x_res[:, :, :], ALU.add)\
                    .then_inc(out_added, 1)

        @block.scalar
        def _(act):
            A = act.activation

            def root(k):
                act.wait_ge(var_ready, k + 1)

            for count, src, hi, _ in setup_parts:
                act.wait_ge(setup_mm, count)
                A(hi, src, ACT.Copy).then_inc(setup_hi, 1)

            act.sem_inc(y1_stored, BATCH)
            with act.Fori(0, NCH) as j:
                for b in range(BATCH):
                    act.wait_ge(conv1_done, j * BATCH + b + 1)
                    A(chunk_of(b, j), ps[:, b, 0:CHUNK], ACT.Identity, bias=c1("b1"))\
                        .then_inc(y1_stored, 1)
            root(0)
            A(c1("sd"), c1("var"), ACT.Sqrt).then_inc(sd_ready, 1)
            act.wait_ge(bn1_ready, 1)
            with act.Fori(0, NCH) as j:
                for b in range(BATCH):
                    act.wait_ge(y1_split, j * BATCH + b + 1)
                    A(y1_f[:, b], chunk_of(b, j), ACT.Relu, bias=c1("bias1"), scale=c1("scale1"))\
                        .then_inc(y1_act, 1)
            act.sem_inc(y2_stored, BATCH)
            with act.Fori(0, NCH) as j:
                for b in range(BATCH):
                    act.wait_ge(conv2_done, j * BATCH + b + 1)
                    A(chunk_of(b, j), ps[:, b, 0:CHUNK], ACT.Identity, bias=c1("b2"))\
                        .then_inc(y2_stored, 1)
            root(1)
            A(c1("sd"), c1("var"), ACT.Sqrt).then_inc(sd_ready, 1)
            act.wait_ge(bn2_ready, 1)
            with act.Fori(0, NCH) as j:
                for b in range(BATCH):
                    A(chunk_of(b, j), chunk_of(b, j), ACT.Relu, bias=c1("bias2"), scale=c1("scale2"))\
                        .then_inc(y2_act, 1)
            act.wait_ge(y2_mean, 1)
            act.sem_inc(y2_turned, BATCH)
            with act.Fori(0, NCH) as j:
                for b in range(BATCH):
                    act.wait_ge(y2_turned, j * BATCH + b + 1)
                    A(y2_c[:, b], chunk_of(b, j), ACT.Identity, bias=c1("neg_mean2"))\
                        .then_inc(y2_centred, 1)
            root(2)
            A(tmp[2][:, :], tmp[1][:, :], ACT.Sqrt).then_inc(sd_ready, 1)

            act.wait_ge(cov_ready, 1)
            act.sem_inc(act_read, N_ACT)
            with act.Fori(0, NCH) as j:
                for b in range(BATCH):
                    n = j * BATCH + b
                    for k, p in enumerate(BY_ACT):
                        act.wait_ge(z_done, n * PATHS + p + 1)
                        if k >= 2:
                            act.wait_ge(pool_added, n * N_ACT + k - 1)
                        elif True:
                            act.wait_ge(pool_added, n * N_ACT)
                        s = 2 * (p % PAIRRING)
                        A(act_out[k % 2][:, :, :], ps[:, s:s + 2, 0:CHUNK], ACT.Relu)\
                            .then_inc(act_read, 1)
            for k in range(HALVES):
                root(3 + k)
                A(c1(f"sd4_{k}"), c1(f"var4_{k}"), ACT.Sqrt).then_inc(sd_ready, 1)

            act.wait_ge(bn4_ready, 1)
            with act.Fori(0, BATCH) as b:
                units = proj_units()
                at = 0
                for q, w in enumerate(PIECES):
                    act.wait_ge(xp_loaded[q % 2], b * 32 + (q // 2 + 1) * 16)
                    for k in range(HALVES):
                        A(xp_f[q % 2][:, k, 0:w], xp_f[q % 2][:, k, 0:w], ACT.Identity,
                          bias=c1("bias4", 2)[:, k:k + 1], scale=c1("scale4", 2)[:, k:k + 1])\
                            .then_inc(xp_normed, 1)
                    for u in (u for u in units if u[0] == q - 1):
                        act.wait_ge(proj_done, b * UNITS + at + 1)
                        A(u[2], ps_unit(at, u), ACT.Copy).then_inc(proj_hi, 1)
                        at += 1
                for u in (u for u in units if u[0] == len(PIECES) - 1):
                    act.wait_ge(proj_done, b * UNITS + at + 1)
                    A(u[2], ps_unit(at, u), ACT.Copy).then_inc(proj_hi, 1)
                    at += 1

                def evac(n, i, free):
                    m = MT[i]
                    act.wait_ge(qk_done, n * NMT + i + 1)
                    act.wait_ge(sub_done, free)
                    A(scores[0:m, i], ps[0:m, i % SRING, 0:CHUNK], ACT.Copy).then_inc(s_evac, 1)

                def stage(g, ahead):
                    for i in range(NMT):
                        m = MT[i]
                        act.wait_ge(sub_done, g * NMT + i + 1)
                        A(p_f[0:m, i % PRING], p_f[0:m, i % PRING], ACT.Exp).then_inc(exp_done, 1)
                        if ahead:
                            evac(g + 1, i, g * NMT + i + 1)
                        act.wait_ge(exp_done, g * NMT + i + 1)
                        if i == 0 or i >= PRING:
                            act.wait_ge(pv_done, g * NMT + (i - PRING + 1 if i else 0))
                        A(p_hi[0:m, i % PRING], p_f[0:m, i % PRING], ACT.Copy).then_inc(hi_done, 1)
                        if i == NMT // 2:
                            act.wait_ge(xr_loaded, g * 16 + 16)
                            for k in range(HALVES):
                                A(x_res[:, k], x_res[:, k], ACT.Identity,
                                  bias=c1("bias4", 2)[:, k:k + 1],
                                  scale=c1("scale4", 2)[:, k:k + 1]).then_inc(xr_normed, 1)

                for i in range(NMT):
                    evac(b * NCH, i, b * NCH * NMT)
                with act.Fori(0, NCH - 1) as j:
                    stage(b * NCH + j, True)
                stage(b * NCH + NCH - 1, False)

        @block.vector
        def _(dve):
            chain = [0]

            def link(ins):
                chain[0] += 1
                ins.then_inc(dve_step, 1)
                dve.wait_ge(dve_step, chain[0])

            def copy(dst, src):
                return dve.tensor_copy(dst, src)

            dve.wait_ge(consts_made, 6)
            dve.wait_ge(weights_loaded, 16 * N_WEIGHTS)
            link(dve.tensor_tensor(
                taps_f[:, :, :].rearrange("p t (a i) -> p t a i", i=HDIM),
                w2_n[:, :].rearrange("p (i t) -> p t i", t=TAPS).unsqueeze(2)
                .to_broadcast([PART, TAPS, PATHS, HDIM]),
                groups[:, :].rearrange("p (a i) -> p a i", i=HDIM).unsqueeze(1)
                .to_broadcast([PART, TAPS, PATHS, HDIM]), ALU.mult))
            dve.sem_inc(taps_made, 1)
            dve.memset(zero, 0.0).then_inc(zero_made, 1)
            dve.wait_ge(setup_mm, 8)
            copy(w1_t[:, :, :], ps[:, 0, 0:HALVES * PART].rearrange("p (k n) -> p k n", k=HALVES))\
                .then_inc(dve_step, 1)
            copy(w3_t[:, :], ps[:, 1, 0:CIN]).then_inc(dve_step, 1)
            copy(c1("gamma"), ps[:, 7, 0:1]).then_inc(dve_step, 1)
            chain[0] += 3
            for k, (_, src, hi, lo) in enumerate(setup_parts):
                dve.wait_ge(setup_hi, k + 1)
                dve.tensor_tensor(lo, src, hi.bitcast(F32), ALU.subtract).then_inc(dve_step, 1)
                chain[0] += 1
            dve.wait_ge(dve_step, chain[0])
            dve.sem_inc(setup_done, 1)

            def per_chunk_stats(stored, seeded, counted):
                with dve.Fori(0, NCH) as j:
                    for b in range(BATCH):
                        dve.wait_ge(stored, j * BATCH + b + 1 + seeded)
                        dve.bn_stats(stats_at(0, j * BATCH + b), chunk_of(b, j)).then_inc(counted, 1)

            def stats_at(k, n):
                return stats[:, k, bass.ds(n, 1)].rearrange("p o s -> p (o s)")

            def bn_coefs(k, stats_k, g, be, scale, bias, var, sd, nth, mv):
                link(dve.bn_aggr(mv, stats_k))
                link(dve.tensor_scalar(var, mv[:, 1:2], EPS, None, ALU.add))
                dve.sem_inc(var_ready, 1)
                dve.wait_ge(sd_ready, nth + 1)
                link(dve.reciprocal(sd, sd))
                link(dve.tensor_tensor(scale, g, sd, ALU.mult))
                link(dve.tensor_tensor(c1("mean_scale"), mv[:, 0:1], scale, ALU.mult))
                link(dve.tensor_tensor(bias, be, c1("mean_scale"), ALU.subtract))

            all_stats = stats[:, 0].rearrange("p n s -> p (n s)")
            per_chunk_stats(y1_stored, BATCH, y1_stats)
            dve.wait_ge(y1_stats, NALL)
            bn_coefs(0, all_stats, c1("g1"), c1("be1"), c1("scale1"), c1("bias1"), c1("var"),
                     c1("sd"), 0, mean_var[:, 0])
            dve.sem_inc(bn1_ready, 1)
            dve.wait_ge(pad_zeroed, 2)
            dve.sem_inc(y1_split, BATCH)
            with dve.Fori(0, NCH) as j:
                for b in range(BATCH):
                    dve.wait_ge(y1_act, j * BATCH + b + 1)
                    src = y1_f[:, b].rearrange("p (r c) -> p r c", c=IMG)
                    copy(padded(y1_hi, b, j * ROWS + 1, ROWS, 1), src).then_inc(y1_hi_done, 1)
                    dve.wait_ge(y1_hi_done, j * BATCH + b + 1)
                    dve.tensor_tensor(padded(y1_lo, b, j * ROWS + 1, ROWS, 1), src,
                                      padded(y1_hi, b, j * ROWS + 1, ROWS, 1).bitcast(F32),
                                      ALU.subtract).then_inc(y1_split, 1)
            per_chunk_stats(y2_stored, BATCH, y2_stats)
            dve.wait_ge(y2_stats, NALL)
            bn_coefs(0, all_stats, c1("g2"), c1("be2"), c1("scale2"), c1("bias2"), c1("var"),
                     c1("sd"), 1, mean_var[:, 0])
            dve.sem_inc(bn2_ready, 1)
            with dve.Fori(0, NCH) as j:
                for b in range(BATCH):
                    n = j * BATCH + b
                    dve.wait_ge(y2_act, n + 1)
                    dve.bn_stats(stats_at(0, n), chunk_of(b, j)).then_inc(y2_stats, 1)
            dve.wait_ge(y2_stats, 2 * NALL)
            link(dve.bn_aggr(mean_var[:, 0], all_stats))
            link(dve.tensor_scalar(c1("neg_mean2"), mean_var[:, 0, 0:1], -1.0, None, ALU.mult))
            dve.sem_inc(y2_mean, 1)
            dve.sem_inc(y2_t_ready, BATCH)
            with dve.Fori(0, NCH) as j:
                for b in range(BATCH):
                    n = j * BATCH + b
                    copy(y2_hi[:, b, bass.ds(j * CHUNK, CHUNK)], chunk_of(b, j))\
                        .then_inc(y2_hi_done, 1)
                    dve.wait_ge(y2_turned, BATCH + n + 1)
                    dve.wait_ge(gram_free, n + 1)
                    copy(y2t_slot(b), ps[0:QSUB, b, :]).then_inc(y2_t_ready, 1)
                    dve.wait_ge(y2_hi_done, n + 1)
                    dve.tensor_tensor(y2_lo[:, b, bass.ds(j * CHUNK, CHUNK)], chunk_of(b, j),
                                      y2_hi[:, b, bass.ds(j * CHUNK, CHUNK)].bitcast(F32),
                                      ALU.subtract).then_inc(y2_split, 1)
            cov, wcov, wmean = tmp[0], tmp[1], tmp[3]
            dve.wait_ge(gram_done, 1)
            link(dve.scalar_tensor_tensor(cov[:, 0:PART], ps[:, 4, 0:PART], 1.0 / TOTAL,
                                          groups[:, :], ALU.mult, ALU.mult))
            link(dve.tensor_scalar(wmean[:, :], w3_t[:, :], mean_var[:, 0, 0:1], None, ALU.mult))
            dve.sem_inc(cov_ready, 1)
            dve.wait_ge(wcov_done, 1)
            link(dve.tensor_tensor(wcov[:, :], ps[:, 5, 0:CIN], w3_t[:, :], ALU.mult))
            dve.sem_inc(cov_ready, 1)
            dve.wait_ge(wcov_done, 2)
            link(dve.tensor_scalar(tmp[1][:, :], ps[:, 6, 0:CIN], 0.0, EPS, ALU.max, ALU.add))
            dve.sem_inc(var_ready, 1)
            link(dve.tensor_tensor(tmp[4][:, :], ps[:, 7, 0:CIN], b3_b[:, :], ALU.add))
            link(dve.tensor_tensor(tmp[5][:, :], b3_b[:, :], tmp[4][:, :], ALU.subtract))
            dve.wait_ge(sd_ready, 3)
            link(dve.reciprocal(tmp[1][:, :], tmp[2][:, :]))
            link(dve.tensor_tensor(tmp[2][:, :], tmp[1][:, :], g3_b[:, :], ALU.mult))
            link(dve.tensor_tensor(tmp[3][:, :], w3_t[:, :], tmp[2][:, :], ALU.mult))
            link(copy(ws_hi[:, :], tmp[3][:, :]))
            link(dve.tensor_tensor(ws_lo[:, :], tmp[3][:, :], ws_hi[:, :].bitcast(F32),
                                   ALU.subtract))
            link(dve.tensor_tensor(tmp[4][:, :], tmp[5][:, :], tmp[2][:, :], ALU.mult))
            link(dve.tensor_tensor(tmp[5][:, :], tmp[4][:, :], be3_b[:, :], ALU.add))
            link(copy(bias_hi[:, :], tmp[5][:, :]))
            link(dve.tensor_tensor(bias_lo[:, :], tmp[5][:, :], bias_hi[:, :].bitcast(F32),
                                   ALU.subtract))
            dve.sem_inc(bias_ready, 1)
            for r, t in ((0, ws_hi), (2, ws_lo)):
                for g in range(BLOCKS):
                    rows = slice(g * BROWS, (g + 1) * BROWS)
                    link(dve.tensor_tensor(
                        path_w[r * BROWS:(r + 1) * BROWS, g * BPATHS:(g + 1) * BPATHS, :],
                        t[rows, :].bitcast(F32).unsqueeze(1)
                        .to_broadcast([BROWS, BPATHS, CIN]),
                        groups[rows, g * BROWS:(g + 1) * BROWS:HDIM].unsqueeze(2)
                        .to_broadcast([BROWS, BPATHS, CIN]), ALU.mult))
                if r == 0:
                    dve.sem_inc(path_w_ready, 1)
            dve.sem_inc(path_w_ready, 1)

            by_dve = [p for p in range(PATHS) if p not in BY_ACT]
            dve.sem_inc(dve_read, N_DVE)
            dve.sem_inc(s_ready, 2)
            with dve.Fori(0, NCH) as j:
                for b in range(BATCH):
                    n = j * BATCH + b
                    for k, p in enumerate(by_dve):
                        dve.wait_ge(z_done, n * PATHS + p + 1)
                        s, acc = 2 * (p % PAIRRING), dve_sum[k % 2][:, :, :]
                        z = ps[:, s:s + 2, 0:CHUNK]
                        if k < 2:
                            dve.wait_ge(s_ready, n + 2)
                            dve.tensor_scalar(acc, z, 0.0, None, ALU.max).then_inc(dve_read, 1)
                        else:
                            dve.wait_ge(dve_read, (n + 1) * N_DVE + k - 1)
                            dve.scalar_tensor_tensor(acc, z, 0.0, acc, ALU.max, ALU.add)\
                                .then_inc(dve_read, 1)
                    dve.wait_ge(dve_read, (n + 2) * N_DVE)
                    dve.tensor_tensor(dve_sum[0][:, :, :], dve_sum[0][:, :, :],
                                      dve_sum[1][:, :, :], ALU.add).then_inc(dve_added, 1)
                    dve.wait_ge(dve_added, n + 1)
                    dve.wait_ge(pool_added, (n + 1) * N_ACT)
                    dve.wait_ge(s_stored[b % 2], (j * 2 + b // 2) * 16)
                    dve.wait_ge(s_stats, n * HALVES)
                    dve.tensor_tensor(s_out[b % 2][:, :, :], dve_sum[0][:, :, :],
                                      pool_sum[b % 2][:, :, :], ALU.add).then_inc(s_ready, 1)
                    dve.wait_ge(s_ready, 2 + n + 1)
                    for k in range(HALVES):
                        dve.bn_stats(stats_at(k, n), s_out[b % 2][:, k]).then_inc(s_stats, 1)
            dve.wait_ge(s_stats, NALL * HALVES)
            for k in range(HALVES):
                bn_coefs(k, stats[:, k].rearrange("p n s -> p (n s)"), c1("g4", 2)[:, k:k + 1],
                         c1("be4", 2)[:, k:k + 1], c1("scale4", 2)[:, k:k + 1],
                         c1("bias4", 2)[:, k:k + 1], c1(f"var4_{k}"), c1(f"sd4_{k}"), 3 + k,
                         mean_var[:, k])
            dve.sem_inc(bn4_ready, 1)

            dve.sem_inc(proj_lo, USLACK)

            def prep(g, slot):
                dve.wait_ge(xq_loaded, g * 16 + 16)
                for k in range(HALVES):
                    dve.tensor_scalar(slot(xq_f)[:, k], slot(xq_f)[:, k],
                                      c1("scale4", 2)[:, k:k + 1], c1("bias4", 2)[:, k:k + 1],
                                      ALU.mult, ALU.add).then_inc(xq_step, 1)
                dve.wait_ge(xq_step, g * 3 + 2)
                copy(slot(xq_hi), slot(xq_f)).then_inc(xq_step, 1)
                dve.wait_ge(xq_step, g * 3 + 3)
                dve.tensor_tensor(slot(xq_lo), slot(xq_f), slot(xq_hi).bitcast(F32), ALU.subtract)\
                    .then_inc(xq_split, 1)

            prep(0, lambda t: t[:, 0])
            prep(1, lambda t: t[:, 1])

            with dve.Fori(0, BATCH) as b:
                units = proj_units()
                at = 0

                def lows(q, at):
                    for u in (u for u in units if u[0] == q):
                        dve.wait_ge(proj_hi, b * UNITS + at + 1)
                        dve.tensor_tensor(u[3], ps_unit(at, u), u[2].bitcast(F32), ALU.subtract)\
                            .then_inc(proj_lo, 1)
                        at += 1
                    return at

                for q, w in enumerate(PIECES):
                    n = b * len(PIECES) + q
                    dve.wait_ge(xp_normed, n * HALVES + HALVES)
                    if q >= 2:
                        dve.wait_ge(proj_done, b * UNITS + sum(u[0] <= q - 2 for u in units))
                    i = q % 2
                    copy(xp_hi[i][:, :, 0:w], xp_f[i][:, :, 0:w]).then_inc(xp_hi_done, 1)
                    dve.wait_ge(xp_hi_done, n + 1)
                    dve.tensor_tensor(xp_lo[i][:, :, 0:w], xp_f[i][:, :, 0:w],
                                      xp_hi[i][:, :, 0:w].bitcast(F32), ALU.subtract)\
                        .then_inc(xp_split, 1)
                    if q:
                        at = lows(q - 1, at)
                lows(len(PIECES) - 1, at)

                def running_max(n, i):
                    if i == 0:
                        return
                    m = MT[i]
                    dve.wait_ge(s_evac, n * NMT + i + 1)
                    if i > 1:
                        dve.wait_ge(max_done, n * (NMT - 1) + i - 1)
                    dve.tensor_tensor(row_max[0:m, :], scores[0:m, i],
                                      scores[0:m, 0] if i == 1 else row_max[0:m, :], ALU.max)\
                        .then_inc(max_done, 1)

                def low(g, i):
                    m = MT[i]
                    dve.wait_ge(hi_done, g * NMT + i + 1)
                    dve.tensor_tensor(p_lo[0:m, i % PRING], p_f[0:m, i % PRING],
                                      p_hi[0:m, i % PRING].bitcast(F32), ALU.subtract)\
                        .then_inc(lo_done, 1)

                def stage(g, ahead):
                    dve.wait_ge(max_turned, g + 1)
                    dve.tensor_reduce(max_q[:, :],
                                      ps[0:QSUB, BANK_MAX, :].rearrange("p (a n) -> p a n", a=4),
                                      AX.X, ALU.max).then_inc(maxq_done, 1)
                    dve.wait_ge(maxq_done, g + 1)
                    dve.tensor_tensor(
                        diag[:, :, :],
                        ident[0:QSUB, 0:QSUB].unsqueeze(1).to_broadcast([QSUB, 4, QSUB]),
                        max_q[:, :].unsqueeze(2).to_broadcast([QSUB, 4, QSUB]),
                        ALU.mult).then_inc(diag_done, 1)
                    dve.wait_ge(maxb_done, g + 1)
                    dve.wait_ge(o_read, g * HALVES)
                    copy(max_b[:, :], ps[:, BANK_MAX, 0:CHUNK]).then_inc(maxb_ready, 1)
                    dve.wait_ge(maxb_ready, g + 1)
                    for i in range(NMT + 2):
                        if i < NMT:
                            m = MT[i]
                            if i == 0 or i >= PRING:
                                k = i - PRING + 1 if i else 0
                                dve.wait_ge(lo_done, g * NMT + k)
                                dve.wait_ge(sum_added, g * (NMT - 1) + (max(1, k - 1) if i else 0))
                            dve.tensor_tensor(p_f[0:m, i % PRING], scores[0:m, i], max_b[0:m, :],
                                              ALU.subtract).then_inc(sub_done, 1)
                        if ahead and 1 <= i <= NMT:
                            running_max(g + 1, i - 1)
                        if i >= 2:
                            low(g, i - 2)
                        if i == NMT // 2:
                            prep(g + 2, lambda t: xq_slot(t, g % 2))
                    dve.wait_ge(l_done, g + 1)
                    dve.wait_ge(sub_done, g * NMT + NMT)
                    dve.reciprocal(recip_b[:, :], ps[:, BANK_SUM, 0:CHUNK]).then_inc(linv_done, 1)
                    dve.wait_ge(linv_done, g + 1)
                    dve.wait_ge(pv_done, g * NMT + NMT)
                    dve.wait_ge(out_stored, g * 16)
                    for k in range(HALVES):
                        dve.scalar_tensor_tensor(
                            o_buf[:, k], ps[:, BANK_O + k, 0:CHUNK], c1("gamma"), recip_b[:, :],
                            ALU.mult, ALU.mult).then_inc(o_read, 1)

                for i in range(NMT):
                    running_max(b * NCH, i)
                with dve.Fori(0, NCH - 1) as j:
                    stage(b * NCH + j, True)
                stage(b * NCH + NCH - 1, False)

        @block.tensor
        def _(pe):
            def mm(out, lhsT, rhs, start=True, stop=True):
                return nc.tensor.matmul(out, lhsT, rhs, start=start, stop=stop)

            def products(out, pairs, first=True, last=True):
                for n, (lhsT, rhs) in enumerate(pairs):
                    ins = mm(out, lhsT, rhs, start=first and n == 0,
                             stop=last and n == len(pairs) - 1)
                return ins

            pe.wait_ge(consts_made, 6)
            pe.wait_ge(weights_loaded, 16 * N_WEIGHTS)
            for k in range(HALVES):
                ins = nc.tensor.transpose(ps[:, 0, k * PART:(k + 1) * PART],
                                          w1_n[:, k * PART:(k + 1) * PART], ident[:, :])
            ins.then_inc(setup_mm, 1)
            for k in range(HALVES):
                ins = nc.tensor.transpose(ps[:, 1, k * PART:(k + 1) * PART], w3_n[:, k, :],
                                          ident[:, :])
            ins.then_inc(setup_mm, 1)
            for k in range(HALVES):
                for q in range(HALVES):
                    ins = mm(ps[:, 5, k * CIN:(k + 1) * CIN], wk_n[:, q, k * PART:(k + 1) * PART],
                             wq_n[:, q, :], start=q == 0, stop=q == HALVES - 1)
            ins.then_inc(setup_mm, 1)
            for k in range(HALVES):
                for q in range(HALVES):
                    at = k * CIN + q * PART
                    ins = nc.tensor.transpose(ps[:, 6, at:at + PART],
                                              wv_n[:, q, k * PART:(k + 1) * PART], ident[:, :])
            ins.then_inc(setup_mm, 1)
            mm(ps[:, 7, 0:1], ones[0:1, :], gamma_row[:, :]).then_inc(setup_mm, 1)
            pe.wait_ge(taps_made, 1)
            for t in range(TAPS):
                ins = nc.tensor.transpose(ps[:, 2 + t // 4, (t % 4) * PART:(t % 4 + 1) * PART],
                                          taps_f[:, t, :], ident[:, :])
                if t % 4 == 3 or t == TAPS - 1:
                    ins.then_inc(setup_mm, 1)

            pe.wait_ge(setup_done, 1)
            with pe.Fori(0, NCH) as j:
                for b in range(BATCH):
                    pe.wait_ge(x_loaded[b], j * 16 + 16)
                    pe.wait_ge(y1_stored, j * BATCH + b + 1)
                    products(ps[:, b, 0:CHUNK], [(w1_t[:, k], x_ring[:, b, k])
                                                 for k in range(HALVES)]).then_inc(conv1_done, 1)

            def conv2(j, b, rows_ready):
                pe.wait_ge(y1_split, BATCH + rows_ready)
                pe.wait_ge(y2_stored, j * BATCH + b + 1)
                pairs = []
                for t in range(TAPS):
                    dy, dx = divmod(t, 3)
                    hi = padded(y1_hi, b, j * ROWS + dy, ROWS, dx)
                    lo = padded(y1_lo, b, j * ROWS + dy, ROWS, dx)
                    pairs += [(taps_hi[:, t], hi), (taps_hi[:, t], lo), (taps_lo[:, t], hi)]
                out = ps[:, b, 0:CHUNK].rearrange("p (r c) -> p r c", c=IMG)
                products(out, pairs).then_inc(conv2_done, 1)

            with pe.Fori(0, NCH - 1) as j:
                for b in range(BATCH):
                    conv2(j, b, (j + 1) * BATCH + b + 1)
            for b in range(BATCH):
                conv2(NCH - 1, b, NALL)

            gram = ps[:, 4, 0:PART]
            pe.wait_ge(zero_made, 1)
            mm(gram, zero, zero, start=True, stop=False)
            pe.sem_inc(gram_free, 2)
            with pe.Fori(0, NCH) as j:
                def turn(b):
                    pe.wait_ge(y2_centred, j * BATCH + b + 1)
                    pe.wait_ge(y2_t_ready, j * BATCH + b + 1)
                    for q in range(4):
                        ins = nc.tensor.transpose(ps[0:QSUB, b, q * PART:(q + 1) * PART],
                                                  y2_c[:, b, q * QSUB:(q + 1) * QSUB], ident[:, :])
                    ins.then_inc(y2_turned, 1)

                def gram_of(b):
                    pe.wait_ge(y2_t_ready, BATCH + j * BATCH + b + 1)
                    for q in range(4):
                        piece = y2t_slot(b)[:, q * PART:(q + 1) * PART]
                        ins = mm(gram, piece, piece, start=False, stop=False)
                    ins.then_inc(gram_free, 1)

                turn(0)
                for b in range(1, BATCH):
                    turn(b)
                    gram_of(b - 1)
                gram_of(BATCH - 1)
            mm(gram, zero, zero, start=False, stop=True).then_inc(gram_done, 1)
            pe.wait_ge(cov_ready, 1)
            mm(ps[:, 5, 0:CIN], tmp[0][:, 0:PART], w3_t[:, :]).then_inc(wcov_done, 1)
            mm(ps[:, 7, 0:CIN], groups[:, :], tmp[3][:, :])
            pe.wait_ge(cov_ready, 2)
            mm(ps[:, 6, 0:CIN], groups[:, :], tmp[1][:, :]).then_inc(wcov_done, 1)

            pe.wait_ge(path_w_ready, 2)
            pe.wait_ge(path_rows_copied, 48)
            with pe.Fori(0, NCH) as j:
                for b in range(BATCH):
                    n = j * BATCH + b
                    pe.wait_ge(staged_in[b % 2], (j * 2 + b // 2 + 1) * 16 * 3 * BLOCKS)
                    for p in range(PATHS):
                        last = (p - PAIRRING) % PATHS
                        round_ = n if p < PAIRRING else n + 1
                        if last in BY_ACT:
                            pe.wait_ge(act_read, round_ * N_ACT + BY_ACT.index(last) + 1)
                        else:
                            done = sum(q not in BY_ACT for q in range(last + 1))
                            pe.wait_ge(dve_read, round_ * N_DVE + done)
                        s = 2 * (p % PAIRRING)
                        for k in range(HALVES):
                            ins = mm(ps[:, s + k, 0:CHUNK], path_w[:, p, k * PART:(k + 1) * PART],
                                     staged[b % 2][p // BPATHS][:, :])
                        ins.then_inc(z_done, 1)

            with pe.Fori(0, BATCH) as b:
                pe.wait_ge(s_evac, b * NCH * NMT)
                for at, u in enumerate(proj_units()):
                    q = u[0]
                    pe.wait_ge(xp_split, b * len(PIECES) + q + 1)
                    pe.wait_ge(proj_lo, b * UNITS + at + 1)
                    products(ps_unit(at, u), u[1]).then_inc(proj_done, 1)
                pe.wait_ge(proj_lo, b * UNITS + UNITS + USLACK)

                def qk(n, i):
                    if i == 0:
                        pe.wait_ge(xq_split, n + 1)
                        pe.wait_ge(s_evac, n * NMT)
                    elif i >= SRING:
                        pe.wait_ge(s_evac, n * NMT + i - SRING + 1)
                    keys = slice(MOFF[i], MOFF[i] + MT[i])
                    pairs = []
                    for k in range(HALVES):
                        xh, xl = (xq_slot(t, n % 2)[:, k] for t in (xq_hi, xq_lo))
                        pairs += [(t_hi[:, k, keys], xh), (t_hi[:, k, keys], xl),
                                  (t_lo[:, k, keys], xh)]
                    products(ps[0:MT[i], i % SRING, 0:CHUNK], pairs).then_inc(qk_done, 1)

                def pv(g, i):
                    m, r = MT[i], i % PRING
                    pe.wait_ge(lo_done, g * NMT + i + 1)
                    if i == 0:
                        pe.wait_ge(o_read, g * HALVES)
                    for k in range(HALVES):
                        c = slice(k * PART, (k + 1) * PART)
                        ins = products(ps[:, BANK_O + k, 0:CHUNK],
                                       [(v_hi[0:m, i, c], p_hi[0:m, r]),
                                        (v_hi[0:m, i, c], p_lo[0:m, r]),
                                        (v_lo[0:m, i, c], p_hi[0:m, r])],
                                       first=i == 0, last=i == NMT - 1)
                    ins.then_inc(pv_done, 1)

                def turn_max(n):
                    pe.wait_ge(max_done, n * (NMT - 1) + NMT - 1)
                    pe.wait_ge(maxb_ready, n)
                    for q in range(4):
                        ins = nc.tensor.transpose(
                            ps[0:QSUB, BANK_MAX, q * PART:(q + 1) * PART],
                            row_max[:, q * QSUB:(q + 1) * QSUB], ident[:, :])
                    ins.then_inc(max_turned, 1)

                def spread_max(g):
                    pe.wait_ge(diag_done, g + 1)
                    mm(ps[:, BANK_MAX, 0:CHUNK], ones[0:QSUB, :],
                       diag[:, :, :].rearrange("p a n -> p (a n)")).then_inc(maxb_done, 1)

                def sum_up(g):
                    pe.wait_ge(sum_added, g * (NMT - 1) + NMT - 1)
                    pe.wait_ge(o_read, g * HALVES)
                    mm(ps[:, BANK_SUM, 0:CHUNK], ones[:, :], p_sum[:, :]).then_inc(l_done, 1)

                def stage(g, ahead):
                    for i in range(NMT + LAG):
                        if ahead and i < NMT:
                            qk(g + 1, i)
                        if i == 0:
                            spread_max(g)
                        if ahead and i == NMT + LAG - 1:
                            turn_max(g + 1)
                        if i >= LAG:
                            pv(g, i - LAG)
                    sum_up(g)

                for i in range(NMT):
                    qk(b * NCH, i)
                turn_max(b * NCH)
                with pe.Fori(0, NCH - 1) as j:
                    stage(b * NCH + j, True)
                stage(b * NCH + NCH - 1, False)


_INS = ["x", "L0_conv_w1", "L0_conv_b1", "L0_conv_g1", "L0_conv_be1", "L0_conv_w2", "L0_conv_b2",
        "L0_conv_g2", "L0_conv_be2", "L0_conv_w3", "L0_conv_b3", "L0_conv_g3", "L0_conv_be3",
        "L0_conv_g4", "L0_conv_be4", "L1_conv_Wq", "L1_conv_Wk", "L1_conv_Wv", "L1_conv_gamma"]


def kernel(**inputs):
    import numpy as np
    import concourse.bacc as bacc
    from concourse.bass_utils import run_bass_kernel_spmd

    nc = bacc.Bacc("TRN2", target_bir_lowering=False, num_devices=1)
    arrays, args = {}, []
    for name in _INS:
        a = np.ascontiguousarray(inputs[name])
        arrays[f"in_{name}"] = a
        args.append(nc.dram_tensor(f"in_{name}", a.shape, mybir.dt.from_np(a.dtype),
                                   kind="ExternalInput").ap())
    out = nc.dram_tensor("out", inputs["x"].shape, F32, kind="ExternalOutput").ap()
    conv_attention_kernel(nc, *args, out)
    return run_bass_kernel_spmd(nc, [arrays], core_ids=[0]).results[0]["out"]
```

```python
import concourse.bass as bass
from concourse import mybir

F32 = mybir.dt.float32
F32R = mybir.dt.float32r
ALU = mybir.AluOpType
ACT = mybir.ActivationFunctionType
AX = mybir.AxisListType

PART = 128
BATCH, CIN, IMG = 4, 256, 56
HALVES = CIN // PART
PIX = IMG * IMG
PATHS, HDIM = 32, 4
ROWS = 8
CHUNK = ROWS * IMG
NCH = PIX // CHUNK
NALL = BATCH * NCH
TOTAL = BATCH * PIX
PADW = IMG + 2
TAPS = 9
EPS = 1e-5
BN6 = 6

BLOCKS = 4
BPATHS = PATHS // BLOCKS
BROWS = PART // BLOCKS
KROWS = 3 * BROWS + 2
PAIRRING = 4
N_ACT = 12
BY_ACT = [(2 * k + 1) * PATHS // (2 * N_ACT) for k in range(N_ACT)]
N_DVE = PATHS - N_ACT
ACTRING = 4
FINISH_AFTER = (4, 5)

MT = [PART] * 23 + [96, 96]
NMT = len(MT)
MOFF = [sum(MT[:i]) for i in range(NMT)]
QSUB = CHUNK // 4
SRING = 4
PRING = 3
LAG = 3
AT_SPREAD, AT_SCALE, AT_ADD, AT_RESIDUAL = 4, 8, 12, 20
ONE = 1
PIECE = 2 * CHUNK
PIECES = [PIECE, PIECE, PIECE, CHUNK]
UNITS = sum(2 * (w // CHUNK) for w in PIECES) + NMT
USLACK = 3


def conv_attention_kernel(nc, x, w1, b1, g1, be1, w2, b2, g2, be2, w3, b3, g3, be3, g4, be4,
                          wq, wk, wv, gamma, out):
    x_v = x.rearrange("b (k p) h w -> b p k (h w)", p=PART)
    s_spill = nc.dram_tensor("s_spill", (PART, HALVES, TOTAL), F32, kind="Internal").ap()

    base = (nc.sbuf_base + 31) // 32 * 32
    cursor = [base]

    def place(name, shape, dtype=F32, at=None):
        size = 4
        for n in shape[1:]:
            size *= n
        offset = cursor[0] if at is None else at
        if at is None:
            cursor[0] += (size + 31) // 32 * 32
        return nc.alloc_sbuf_tensor_at(name, list(shape), dtype, offset=offset)

    ident = place("ident", [PART, PART])
    ones = place("ones", [PART, PART])
    groups = place("groups", [PART, PART])
    at_hi = place("at_hi", [PART, HALVES, CIN], F32R)
    at_lo = place("at_lo", [PART, HALVES, CIN], F32R)
    wv_hi = place("wv_hi", [PART, HALVES, CIN], F32R)
    wv_lo = place("wv_lo", [PART, HALVES, CIN], F32R)
    vec = place("vec", [PART, 64])
    col = {}

    def c1(name, n=1):
        if name not in col:
            col[name] = (sum(w for _, w in col.values()), n)
            assert sum(w for _, w in col.values()) <= 64
        at, w = col[name]
        return vec[:, at:at + w]

    mean_var = place("mean_var", [PART, HALVES, 2])
    gamma_row = place("gamma_row", [1, 1])
    l0_base = cursor[0]

    y_raw = place("y_raw", [PART, BATCH, PIX])
    pad_at = [cursor[0], cursor[0] + BATCH * PADW * PADW * 4]
    y1_hi = place("y1_hi", [PART, BATCH, PADW, PADW], F32R)
    y1_lo = place("y1_lo", [PART, BATCH, PADW, PADW], F32R)
    y2_hi = place("y2_hi", [PART, BATCH, PIX], F32R, at=pad_at[0])
    y2_lo = place("y2_lo", [PART, BATCH, PIX], F32R, at=pad_at[1])
    spare = [p + TOTAL * 4 for p in pad_at]
    stats = place("stats", [PART, HALVES, NALL, BN6])
    bufs_at = cursor[0]
    w1_t = place("w1_t", [PART, HALVES, PART])
    w3_t = place("w3_t", [PART, CIN])
    g3_b = place("g3_b", [PART, CIN])
    be3_b = place("be3_b", [PART, CIN])
    b3_b = place("b3_b", [PART, CIN])
    tmp_at = cursor[0]
    tmp = [place(f"tmp{i}", [PART, CIN]) for i in range(6)]
    ws_hi = place("ws_hi", [PART, CIN], F32R)
    ws_lo = place("ws_lo", [PART, CIN], F32R)
    bias_hi = place("bias_hi", [PART, CIN], F32R)
    bias_lo = place("bias_lo", [PART, CIN], F32R)
    ring_at = cursor[0]
    x_ring = place("x_ring", [PART, BATCH, HALVES, CHUNK])
    y1_f = place("y1_f", [PART, BATCH, CHUNK], at=ring_at)
    y2_c = place("y2_c", [PART, BATCH, CHUNK], at=ring_at)
    y2_t = place("y2_t", [QSUB, 2, 4 * PART], at=ring_at + BATCH * CHUNK * 4)
    taps_f = place("taps_f", [PART, TAPS, PART])
    taps_hi = place("taps_hi", [PART, TAPS, PART], F32R)
    taps_lo = place("taps_lo", [PART, TAPS, PART], F32R)
    l0_end = cursor[0]
    w1_n = place("w1_n", [PART, CIN], at=tmp_at)
    w2_n = place("w2_n", [PART, HDIM * TAPS], at=tmp_at + 1024)
    w3_n = place("w3_n", [PART, HALVES, PATHS * HDIM], at=tmp_at + 2048)
    wq_n = place("wq_n", [PART, HALVES, CIN], at=tmp_at + 4096)
    wk_n = place("wk_n", [PART, HALVES, CIN], at=tmp_at + 6144)
    wv_n = place("wv_n", [PART, HALVES, CIN], at=tmp_at + 8192)
    wide = HALVES * CHUNK * 4
    path_w = place("path_w", [KROWS, PATHS, CIN], F32R, at=l0_base)
    staged = [[place(f"staged{i}_{g}", [KROWS, CHUNK], F32R,
                     at=l0_base + PATHS * CIN * 4 + (i * BLOCKS + g) * CHUNK * 4)
               for g in range(BLOCKS)] for i in range(2)]
    bufs = [place(f"buf{i}", [PART, HALVES, CHUNK], at=bufs_at + i * wide)
            for i in range(6 + ACTRING)]
    assert bufs_at + len(bufs) * wide <= l0_end
    dve_sum, s_out, pool_sum = (bufs[i:i + 2] for i in (0, 2, 4))
    act_out = bufs[6:]
    x_again = [place(f"x_again{i}", [PART, HALVES, CHUNK], at=spare[i]) for i in range(2)]

    cursor[0] = l0_base
    t_hi = place("t_hi", [PART, HALVES, PIX], F32R)
    t_lo = place("t_lo", [PART, HALVES, PIX], F32R)
    v_hi = place("v_hi", [PART, NMT, CIN], F32R)
    v_lo = place("v_lo", [PART, NMT, CIN], F32R)
    scores_at = cursor[0]
    scores = place("scores", [PART, NMT, CHUNK])
    p_f = place("p_f", [PART, PRING, CHUNK])
    p_hi = place("p_hi", [PART, PRING, CHUNK], F32R)
    p_lo = place("p_lo", [PART, PRING, CHUNK], F32R)
    xq_hi = place("xq_hi", [PART, 2, HALVES, CHUNK], F32R)
    xq_lo = place("xq_lo", [PART, 2, HALVES, CHUNK], F32R)
    xq_f = place("xq_f", [PART, 2, HALVES, CHUNK])
    x_res = place("x_res", [PART, HALVES, CHUNK])
    row_max = place("row_max", [PART, CHUNK])
    max_b = place("max_b", [PART, CHUNK])
    p_sum = place("p_sum", [PART, CHUNK])
    o_buf = place("o_buf", [PART, HALVES, CHUNK])
    diag = place("diag", [QSUB, 4, QSUB])
    inv_diag = place("inv_diag", [QSUB, 4, QSUB])
    max_q = place("max_q", [QSUB, 4])
    inv_q = place("inv_q", [QSUB, 4])
    l1_end = cursor[0]
    assert max(l0_end, l1_end) <= nc.sbuf_usable_end, (l0_end, l1_end, nc.sbuf_usable_end)
    xp_f = [place(f"xp_f{i}", [PART, HALVES, PIECE], at=scores_at + i * 3 * HALVES * PIECE * 4)
            for i in range(2)]
    xp_hi = [place(f"xp_hi{i}", [PART, HALVES, PIECE], F32R,
                   at=scores_at + (i * 3 + 1) * HALVES * PIECE * 4) for i in range(2)]
    xp_lo = [place(f"xp_lo{i}", [PART, HALVES, PIECE], F32R,
                   at=scores_at + (i * 3 + 2) * HALVES * PIECE * 4) for i in range(2)]

    ps = nc.alloc_psum_tensor("ps", [PART, 8, 512], F32)
    BANK_O, BANK_MAX, BANK_SUM = 4, 6, 7

    def sem(name):
        return nc.alloc_semaphore(name)

    zero = tmp[5][:, 0:PART]

    def block_weights(engine, r, t, g):
        rows = slice(g * BROWS, (g + 1) * BROWS)
        return engine.tensor_tensor(
            path_w[r * BROWS:(r + 1) * BROWS, g * BPATHS:(g + 1) * BPATHS, :],
            t[rows, :].bitcast(F32).unsqueeze(1).to_broadcast([BROWS, BPATHS, CIN]),
            groups[rows, g * BROWS:(g + 1) * BROWS:HDIM].unsqueeze(2)
            .to_broadcast([BROWS, BPATHS, CIN]), ALU.mult)

    def y2t_slot(b):
        return y2_t[:, b % 2]

    def bank(n, width, parts):
        return ps[:, n, 0:width].rearrange("p (k n) -> p k n", k=parts)

    setup_parts = [(2, bank(5, 2 * CIN, 2), at_hi[:, :, :], at_lo[:, :, :]),
                   (3, bank(6, 2 * CIN, 2), wv_hi[:, :, :], wv_lo[:, :, :])]
    for n, t in enumerate(range(0, TAPS, 4)):
        w = min(4, TAPS - t)
        setup_parts.append((5 + n, bank(2 + n, w * PART, w), taps_hi[:, t:t + w],
                            taps_lo[:, t:t + w]))

    def proj_units():
        units = []
        for q, w in enumerate(PIECES):
            xh, xl = xp_hi[q % 2], xp_lo[q % 2]
            for c in range(w // CHUNK):
                px = slice(c * CHUNK, (c + 1) * CHUNK)
                for h in range(HALVES):
                    o, pairs = slice(h * PART, (h + 1) * PART), []
                    for k in range(HALVES):
                        pairs += [(at_hi[:, k, o], xh[:, k, px]), (at_hi[:, k, o], xl[:, k, px]),
                                  (at_lo[:, k, o], xh[:, k, px])]
                    dst = slice(q * PIECE + c * CHUNK, q * PIECE + (c + 1) * CHUNK)
                    units.append((q, pairs, t_hi[:, h, dst], t_lo[:, h, dst]))
            for i in range(NMT):
                if not q * PIECE <= MOFF[i] < q * PIECE + w:
                    continue
                m, pairs = MT[i], []
                px = slice(MOFF[i] - q * PIECE, MOFF[i] - q * PIECE + m)
                for k in range(HALVES):
                    pairs += [(xh[:, k, px], wv_hi[:, k]), (xh[:, k, px], wv_lo[:, k]),
                              (xl[:, k, px], wv_hi[:, k])]
                units.append((q, pairs, v_hi[0:m, i], v_lo[0:m, i]))
        assert len(units) == UNITS
        return units

    def ps_unit(at, unit):
        rows, width = unit[2].shape[0], unit[2].shape[-1]
        return ps[0:rows, at % SRING, 0:width]

    taps_made = sem("taps_made")
    zero_made = sem("zero_made")
    gram_free = sem("gram_free")
    consts_made = sem("consts_made")
    w1_loaded = sem("w1_loaded")
    w1_turned = sem("w1_turned")
    w1_ready = sem("w1_ready")
    weights_loaded = sem("weights_loaded")
    late_loaded = sem("late_loaded")
    setup_mm = sem("setup_mm")
    setup_hi = sem("setup_hi")
    setup_done = sem("setup_done")
    pad_zeroed = sem("pad_zeroed")
    dve_step = sem("dve_step")
    sd_ready = sem("sd_ready")
    var_ready = sem("var_ready")
    x_loaded = [sem(f"x_loaded{b}") for b in range(BATCH)]
    conv1_done = sem("conv1_done")
    y1_stored = sem("y1_stored")
    y1_stats = sem("y1_stats")
    bn1_ready = sem("bn1_ready")
    y1_act = sem("y1_act")
    y1_hi_done = sem("y1_hi_done")
    y1_split = sem("y1_split")
    conv2_done = sem("conv2_done")
    y2_stored = sem("y2_stored")
    y2_stats = sem("y2_stats")
    bn2_ready = sem("bn2_ready")
    y2_act = sem("y2_act")
    y2_mean = sem("y2_mean")
    y2_hi_done = sem("y2_hi_done")
    y2_split = sem("y2_split")
    y2_centred = sem("y2_centred")
    y2_turned = sem("y2_turned")
    y2_t_ready = sem("y2_t_ready")
    gram_done = sem("gram_done")
    cov_ready = sem("cov_ready")
    wcov_done = sem("wcov_done")
    ws_ready = sem("ws_ready")
    path_w_ready = sem("path_w_ready")
    path_w_low = sem("path_w_low")
    path_rows_copied = sem("path_rows_copied")
    bias_ready = sem("bias_ready")
    ones_rows = sem("ones_rows")
    staged_in = [sem(f"staged_in{i}") for i in range(2)]
    x_again_in = [sem(f"x_again_in{i}") for i in range(2)]
    z_done = sem("z_done")
    dve_read = sem("dve_read")
    act_read = sem("act_read")
    pool_added = sem("pool_added")
    dve_added = sem("dve_added")
    s_ready = sem("s_ready")
    s_stats = sem("s_stats")
    s_stored = [sem(f"s_stored{i}") for i in range(2)]
    bn4_ready = sem("bn4_ready")
    xp_loaded = [sem(f"xp_loaded{i}") for i in range(2)]
    xp_normed = sem("xp_normed")
    xp_hi_done = sem("xp_hi_done")
    xp_split = sem("xp_split")
    proj_done = sem("proj_done")
    proj_hi = sem("proj_hi")
    proj_lo = sem("proj_lo")
    xq_loaded = sem("xq_loaded")
    xq_step = sem("xq_step")
    xq_split = sem("xq_split")
    xr_loaded = sem("xr_loaded")
    xr_normed = sem("xr_normed")
    qk_done = sem("qk_done")
    s_evac = sem("s_evac")
    max_done = sem("max_done")
    max_turned = sem("max_turned")
    maxq_done = sem("maxq_done")
    diag_done = sem("diag_done")
    maxb_done = sem("maxb_done")
    maxb_ready = sem("maxb_ready")
    sub_done = sem("sub_done")
    exp_done = sem("exp_done")
    hi_done = sem("hi_done")
    lo_done = sem("lo_done")
    sum_added = sem("sum_added")
    pv_done = sem("pv_done")
    l_done = sem("l_done")
    inv_step = sem("inv_step")
    inv_diag_done = sem("inv_diag_done")
    inv_spread = sem("inv_spread")
    o_evac = sem("o_evac")
    o_scaled = sem("o_scaled")
    out_added = sem("out_added")
    out_stored = sem("out_stored")

    N_WEIGHTS, N_LATE = 10, 18

    def chunk_of(b, j):
        return y_raw[:, b, bass.ds(j * CHUNK, CHUNK)]

    def padded(t, b, row, rows, left):
        return t[:, b, bass.ds(row, rows), left:left + IMG]

    def xq_slot(t, i):
        return t[:, bass.ds(i, 1)].rearrange("p o k n -> p (o k) n")

    def out_at(b, j):
        return out.rearrange("b (k p) h w -> p k b (h w)", p=PART)[
            :, :, bass.ds(b, 1), bass.ds(j * CHUNK, CHUNK)].rearrange("p k o n -> p k (o n)")

    with nc.Block() as block:

        @block.sync
        def _(sp):
            for free in (out_stored, s_stored[0], s_stored[1]):
                sp.sem_inc(free, 16)

            def weight(dst, src, loaded=weights_loaded):
                sp.dma_start(dst, src).then_inc(loaded, 16)

            def column(v):
                return v.rearrange("(p o) -> p o", o=1)

            weight(w1_n[:, :], w1, w1_loaded)
            weight(c1("b1"), column(b1), w1_loaded)
            for b in range(BATCH):
                sp.dma_start(x_ring[:, b], x_v[b][:, :, 0:CHUNK]).then_inc(x_loaded[b], 16)
            weight(w2_n[:, :], w2.rearrange("k i a b -> k (i a b)"))
            for k in range(HALVES):
                weight(w3_n[:, k, :].rearrange("p (a h) -> p a h", h=HDIM),
                       w3[:, k * PART:(k + 1) * PART, :].rearrange("a c h -> c a h"))
            weight(c1("b2"), column(b2))
            weight(c1("g1"), column(g1))
            weight(c1("be1"), column(be1))
            for t, w in ((wq_n, wq), (wk_n, wk), (wv_n, wv)):
                weight(t[:, :, :], w.rearrange("(k p) c -> p k c", p=PART))
            weight(gamma_row[:, :], gamma.rearrange("(p o) -> p o", o=1))
            with sp.Fori(1, NCH) as j:
                for b in range(BATCH):
                    sp.wait_ge(conv1_done, j * BATCH + b - BATCH + 1)
                    sp.dma_start(x_ring[:, b], x_v[b][:, :, bass.ds(j * CHUNK, CHUNK)])\
                      .then_inc(x_loaded[b], 16)

            weight(c1("g2"), column(g2), late_loaded)
            weight(c1("be2"), column(be2), late_loaded)
            for k in range(HALVES):
                half = slice(k * PART, (k + 1) * PART)
                weight(c1("g4", 2)[:, k:k + 1], column(g4[half]), late_loaded)
                weight(c1("be4", 2)[:, k:k + 1], column(be4[half]), late_loaded)
            for t, w in ((g3_b, g3), (be3_b, be3), (b3_b, b3)):
                for h in range(HDIM):
                    weight(t[h:PART:HDIM, :], w, late_loaded)

            def load_chunk(j, b):
                i = b % 2
                for g in range(BLOCKS):
                    rows = slice(g * BROWS, (g + 1) * BROWS)
                    for r, t in ((0, y2_hi), (1, y2_lo), (2, y2_hi)):
                        sp.dma_start(staged[i][g][r * BROWS:(r + 1) * BROWS, :].bitcast(F32),
                                     t[rows, b, bass.ds(j * CHUNK, CHUNK)].bitcast(F32))\
                          .then_inc(staged_in[i], 16)
                sp.dma_start(x_again[i][:, :, :], x_v[b][:, :, bass.ds(j * CHUNK, CHUNK)])\
                  .then_inc(x_again_in[i], 16)

            sp.wait_ge(y2_split, NALL)
            sp.wait_ge(gram_done, 1)
            sp.wait_ge(ones_rows, 2 * BLOCKS)
            load_chunk(0, 0)

            sp.wait_ge(path_w_ready, 1)
            sp.dma_start(path_w[BROWS:2 * BROWS].bitcast(F32), path_w[0:BROWS].bitcast(F32))\
             .then_inc(path_rows_copied, 16)
            sp.wait_ge(bias_ready, 1)
            for r, t in ((0, bias_hi), (1, bias_lo)):
                row = 3 * BROWS + r
                sp.dma_start(path_w[row:row + 1, :, :].bitcast(F32), t[0:PART:HDIM, :].bitcast(F32))\
                  .then_inc(path_rows_copied, 16)

            load_chunk(0, 1)

            def finish(j, b, following):
                sp.wait_ge(s_ready, 2 + j * BATCH + b + 1)
                sp.dma_start(s_spill[:, :, bass.ds(b * PIX + j * CHUNK, CHUNK)],
                             s_out[b % 2][:, :, :]).then_inc(s_stored[b % 2], 16)
                if following:
                    load_chunk(*following)

            with sp.Fori(0, NCH - 1) as j:
                for b in range(BATCH):
                    finish(j, b, (j, b + 2) if b < 2 else (j + 1, b - 2))
            for b in range(BATCH):
                finish(NCH - 1, b, (NCH - 1, b + 2) if b < 2 else None)

            for i in range(2):
                sp.wait_ge(s_stored[i], 16 + 16 * NALL // 2)
            sp.wait_ge(bn4_ready, 1)

            for g in range(2):
                sp.wait_ge(xq_loaded, g * 16)
                sp.dma_start(xq_f[:, g], s_spill[:, :, g * CHUNK:(g + 1) * CHUNK])\
                  .then_inc(xq_loaded, 16)

            def store_out(b, j):
                sp.wait_ge(out_added, ONE + b * NCH + j + 1)
                sp.dma_start(out_at(b, j), o_buf[:, :, :]).then_inc(out_stored, 16)

            def load_for_stage(g):
                sp.wait_ge(xq_split, g + 1)
                sp.wait_ge(xq_loaded, g * 16 + 32)
                n = (g + 2) % NALL
                sp.dma_start(xq_slot(xq_f, g % 2),
                             s_spill[:, :, bass.ds(n * CHUNK, CHUNK)]).then_inc(xq_loaded, 16)

            def load_residual(g):
                sp.wait_ge(out_added, ONE + g)
                sp.dma_start(x_res[:, :, :], s_spill[:, :, bass.ds(g * CHUNK, CHUNK)])\
                  .then_inc(xr_loaded, 16)

            def batch(b, first):
                sp.wait_ge(sub_done, ONE + b * NCH * NMT)
                for q, w in enumerate(PIECES):
                    if q == 2 and not first:
                        store_out(b - 1, NCH - 1)
                    if q >= 2:
                        sp.wait_ge(xp_split, b * len(PIECES) + q - 1)
                    sp.dma_start(xp_f[q % 2][:, :, 0:w],
                                 s_spill[:, :, bass.ds(b * PIX + q * PIECE, w)])\
                      .then_inc(xp_loaded[q % 2], 16)
                load_for_stage(b * NCH)
                load_residual(b * NCH)
                with sp.Fori(1, NCH) as j:
                    load_for_stage(b * NCH + j)
                    store_out(b, j - 1)
                    load_residual(b * NCH + j)

            batch(0, True)
            with sp.Fori(1, BATCH) as b:
                batch(b, False)
            store_out(BATCH - 1, NCH - 1)
            sp.wait_ge(out_stored, 16 + 16 * NALL)
            sp.wait_ge(xq_loaded, 16 * (NALL + 2))

        @block.gpsimd
        def _(pool):
            for free, n in ((pool_added, ACTRING), (sum_added, ONE), (out_added, ONE)):
                pool.sem_inc(free, n)
            pool.memset(ident[:, :], 0.0).then_inc(consts_made, 1)
            pool.memset(ones[:, :], 1.0).then_inc(consts_made, 1)
            pool.memset(groups[:, :], 1.0).then_inc(consts_made, 1)
            pool.wait_ge(consts_made, 3)
            pool.affine_select(out=ident[:, :], in_=ident[:, :], compare_op=ALU.not_equal, fill=1.0,
                               base=0, pattern=[[-1, PART]], channel_multiplier=1)\
                .then_inc(consts_made, 1)
            grid = groups[:, :].rearrange("p (a h) -> p a h", h=HDIM)
            pool.affine_select(out=grid, in_=grid, compare_op=ALU.is_ge, fill=0.0, base=0,
                               pattern=[[-HDIM, PATHS], [0, HDIM]], channel_multiplier=1)\
                .then_inc(consts_made, 1)
            pool.wait_ge(consts_made, 5)
            pool.affine_select(out=grid, in_=grid, compare_op=ALU.is_ge, fill=0.0, base=HDIM - 1,
                               pattern=[[HDIM, PATHS], [0, HDIM]], channel_multiplier=-1)\
                .then_inc(consts_made, 1)
            pool.memset(y1_hi[:, :, :, :].bitcast(F32), 0.0).then_inc(pad_zeroed, 1)
            pool.memset(y1_lo[:, :, :, :].bitcast(F32), 0.0).then_inc(pad_zeroed, 1)

            pool.wait_ge(gram_done, 1)
            for i in range(2):
                for g in range(BLOCKS):
                    pool.memset(staged[i][g][3 * BROWS:KROWS, :].bitcast(F32), 1.0).then_inc(ones_rows, 1)

            pool.wait_ge(ws_ready, 1)
            for g in range(BLOCKS // 2, BLOCKS):
                block_weights(pool, 2, ws_lo, g).then_inc(path_w_low, 1)

            with pool.Fori(0, NCH) as j:
                for b in range(BATCH):
                    i, n = b % 2, j * BATCH + b
                    pool.wait_ge(s_ready, n + 1)
                    for k in range(1, N_ACT):
                        pool.wait_ge(act_read, (n + 1) * N_ACT + k + 1)
                        if k > 1:
                            pool.wait_ge(pool_added, ACTRING + n * (N_ACT - 1) + k - 1)
                        pool.tensor_tensor(pool_sum[i][:, :, :],
                                           act_out[(b * N_ACT + k) % ACTRING][:, :, :],
                                           (act_out[b * N_ACT % ACTRING] if k == 1
                                            else pool_sum[i])[:, :, :],
                                           ALU.add).then_inc(pool_added, 1)

            def add_residual(g):
                pool.wait_ge(o_scaled, (g + 1) * HALVES)
                pool.wait_ge(xr_normed, g * HALVES + HALVES)
                pool.tensor_tensor(o_buf[:, :, :], o_buf[:, :, :], x_res[:, :, :], ALU.add)\
                    .then_inc(out_added, 1)

            def stage(g, late):
                for i in range(1, NMT):
                    m = MT[i]
                    if i == 1:
                        pool.wait_ge(l_done, ONE + g)
                    pool.wait_ge(exp_done, g * NMT + i + 1)
                    if i > 1:
                        pool.wait_ge(sum_added, ONE + g * (NMT - 1) + i - 1)
                    pool.tensor_tensor(p_sum[0:m, :], p_f[0:m, i % PRING],
                                       (p_f[0:m, 0] if i == 1 else p_sum[0:m, :]), ALU.add)\
                        .then_inc(sum_added, 1)
                    if late and i == AT_ADD:
                        add_residual(g - 1)

            with pool.Fori(0, BATCH) as b:
                stage(b * NCH, False)
                with pool.Fori(1, NCH) as j:
                    stage(b * NCH + j, True)
                add_residual(b * NCH + NCH - 1)

        @block.scalar
        def _(act):
            A = act.activation

            def root(k):
                act.wait_ge(var_ready, k + 1)

            for free, n in ((y1_stored, BATCH), (y2_stored, BATCH), (y2_turned, BATCH),
                            (act_read, N_ACT), (s_evac, ONE), (o_evac, ONE)):
                act.sem_inc(free, n)
            act.wait_ge(w1_loaded, 2 * 16)
            with act.Fori(0, NCH) as j:
                for b in range(BATCH):
                    act.wait_ge(conv1_done, j * BATCH + b + 1)
                    A(chunk_of(b, j), ps[:, b, 0:CHUNK], ACT.Identity, bias=c1("b1"))\
                        .then_inc(y1_stored, 1)
            root(0)
            A(c1("sd"), c1("var"), ACT.Sqrt).then_inc(sd_ready, 1)
            for count, src, hi, _ in setup_parts:
                act.wait_ge(setup_mm, count)
                A(hi, src, ACT.Copy).then_inc(setup_hi, 1)

            act.wait_ge(bn1_ready, 1)
            with act.Fori(0, NCH) as j:
                for b in range(BATCH):
                    act.wait_ge(y1_split, j * BATCH + b + 1)
                    A(y1_f[:, b], chunk_of(b, j), ACT.Relu, bias=c1("bias1"), scale=c1("scale1"))\
                        .then_inc(y1_act, 1)
            with act.Fori(0, NCH) as j:
                for b in range(BATCH):
                    act.wait_ge(conv2_done, j * BATCH + b + 1)
                    A(chunk_of(b, j), ps[:, b, 0:CHUNK], ACT.Identity, bias=c1("b2"))\
                        .then_inc(y2_stored, 1)
            root(1)
            A(c1("sd"), c1("var"), ACT.Sqrt).then_inc(sd_ready, 1)
            act.wait_ge(bn2_ready, 1)
            with act.Fori(0, NCH) as j:
                for b in range(BATCH):
                    A(chunk_of(b, j), chunk_of(b, j), ACT.Relu, bias=c1("bias2"), scale=c1("scale2"))\
                        .then_inc(y2_act, 1)
            act.wait_ge(y2_mean, 1)
            with act.Fori(0, NCH) as j:
                for b in range(BATCH):
                    act.wait_ge(y2_turned, j * BATCH + b + 1)
                    A(y2_c[:, b], chunk_of(b, j), ACT.Identity, bias=c1("neg_mean2"))\
                        .then_inc(y2_centred, 1)
            root(2)
            A(tmp[2][:, :], tmp[1][:, :], ACT.Sqrt).then_inc(sd_ready, 1)

            act.wait_ge(ws_ready, 1)
            for p in range(PATHS // 2):
                g = p // BPATHS
                rows = slice(g * BROWS, (g + 1) * BROWS)
                A(path_w[2 * BROWS:3 * BROWS, p, :], ws_lo[rows, :].bitcast(F32), ACT.Identity,
                  scale=groups[rows, p * HDIM:p * HDIM + 1]).then_inc(path_w_low, 1)

            with act.Fori(0, NCH) as j:
                for b in range(BATCH):
                    n = j * BATCH + b
                    for k, p in enumerate(BY_ACT):
                        act.wait_ge(z_done, n * PATHS + p + 1)
                        if k == ACTRING:
                            act.wait_ge(pool_added, ACTRING + n * (N_ACT - 1) + 1)
                        elif k > ACTRING:
                            act.wait_ge(pool_added, ACTRING + n * (N_ACT - 1) + k - ACTRING)
                        else:
                            act.wait_ge(pool_added, n * (N_ACT - 1) + k + 1)
                        s = 2 * (p % PAIRRING)
                        A(act_out[(b * N_ACT + k) % ACTRING][:, :, :], ps[:, s:s + 2, 0:CHUNK],
                          ACT.Relu).then_inc(act_read, 1)
            for k in range(HALVES):
                root(3 + k)
                A(c1(f"sd4_{k}"), c1(f"var4_{k}"), ACT.Sqrt).then_inc(sd_ready, 1)

            act.wait_ge(bn4_ready, 1)
            with act.Fori(0, BATCH) as b:
                units = proj_units()
                at = 0
                for q, w in enumerate(PIECES):
                    act.wait_ge(xp_loaded[q % 2], b * 32 + (q // 2 + 1) * 16)
                    for k in range(HALVES):
                        A(xp_f[q % 2][:, k, 0:w], xp_f[q % 2][:, k, 0:w], ACT.Identity,
                          bias=c1("bias4", 2)[:, k:k + 1], scale=c1("scale4", 2)[:, k:k + 1])\
                            .then_inc(xp_normed, 1)
                    for u in (u for u in units if u[0] == q - 1):
                        act.wait_ge(proj_done, b * UNITS + at + 1)
                        A(u[2], ps_unit(at, u), ACT.Copy).then_inc(proj_hi, 1)
                        at += 1
                for u in (u for u in units if u[0] == len(PIECES) - 1):
                    act.wait_ge(proj_done, b * UNITS + at + 1)
                    A(u[2], ps_unit(at, u), ACT.Copy).then_inc(proj_hi, 1)
                    at += 1

                def evac_out(g):
                    act.wait_ge(pv_done, ONE + (g + 1) * NMT)
                    act.wait_ge(out_stored, 16 + g * 16)
                    for k in range(HALVES):
                        A(o_buf[:, k], ps[:, BANK_O + k, 0:CHUNK], ACT.Copy).then_inc(o_evac, 1)

                def evac(n, i, free):
                    m = MT[i]
                    act.wait_ge(qk_done, n * NMT + i + 1)
                    act.wait_ge(sub_done, ONE + free)
                    A(scores[0:m, i], ps[0:m, i % SRING, 0:CHUNK], ACT.Copy).then_inc(s_evac, 1)

                def stage(g, ahead):
                    for i in range(NMT):
                        m = MT[i]
                        act.wait_ge(sub_done, ONE + g * NMT + i + 1)
                        A(p_f[0:m, i % PRING], p_f[0:m, i % PRING], ACT.Exp).then_inc(exp_done, 1)
                        if ahead:
                            evac(g + 1, i, g * NMT + i + 1)
                        act.wait_ge(exp_done, g * NMT + i + 1)
                        if i == 0 or i >= PRING:
                            act.wait_ge(pv_done, ONE + g * NMT + (i - PRING + 1 if i else 0))
                        A(p_hi[0:m, i % PRING], p_f[0:m, i % PRING], ACT.Copy).then_inc(hi_done, 1)
                        if i == AT_RESIDUAL:
                            act.wait_ge(xr_loaded, g * 16 + 16)
                            for k in range(HALVES):
                                A(x_res[:, k], x_res[:, k], ACT.Identity,
                                  bias=c1("bias4", 2)[:, k:k + 1],
                                  scale=c1("scale4", 2)[:, k:k + 1]).then_inc(xr_normed, 1)
                    evac_out(g)

                for i in range(NMT):
                    evac(b * NCH, i, b * NCH * NMT)
                with act.Fori(0, NCH - 1) as j:
                    stage(b * NCH + j, True)
                stage(b * NCH + NCH - 1, False)

        @block.vector
        def _(dve):
            chain = [0]

            def link(ins):
                chain[0] += 1
                ins.then_inc(dve_step, 1)
                dve.wait_ge(dve_step, chain[0])

            def copy(dst, src):
                return dve.tensor_copy(dst, src)

            for free, n in ((y1_split, BATCH), (y2_t_ready, BATCH), (dve_read, N_DVE),
                            (dve_added, ONE), (s_ready, 2), (proj_lo, USLACK), (maxb_ready, ONE), (sub_done, ONE),
                            (lo_done, ONE)):
                dve.sem_inc(free, n)
            dve.wait_ge(w1_turned, 1)
            copy(w1_t[:, :, :], ps[:, 7, 0:HALVES * PART].rearrange("p (k n) -> p k n", k=HALVES))\
                .then_inc(w1_ready, 1)
            dve.wait_ge(consts_made, 6)
            dve.wait_ge(weights_loaded, 16 * N_WEIGHTS)
            link(dve.tensor_tensor(
                taps_f[:, :, :].rearrange("p t (a i) -> p t a i", i=HDIM),
                w2_n[:, :].rearrange("p (i t) -> p t i", t=TAPS).unsqueeze(2)
                .to_broadcast([PART, TAPS, PATHS, HDIM]),
                groups[:, :].rearrange("p (a i) -> p a i", i=HDIM).unsqueeze(1)
                .to_broadcast([PART, TAPS, PATHS, HDIM]), ALU.mult))
            dve.sem_inc(taps_made, 1)

            def per_chunk_stats(stored, seeded, counted):
                with dve.Fori(0, NCH) as j:
                    for b in range(BATCH):
                        dve.wait_ge(stored, j * BATCH + b + 1 + seeded)
                        dve.bn_stats(stats_at(0, j * BATCH + b), chunk_of(b, j)).then_inc(counted, 1)

            def stats_at(k, n):
                return stats[:, k, bass.ds(n, 1)].rearrange("p o s -> p (o s)")

            def bn_coefs(k, stats_k, g, be, scale, bias, var, sd, nth, mv):
                link(dve.bn_aggr(mv, stats_k))
                link(dve.tensor_scalar(var, mv[:, 1:2], EPS, None, ALU.add))
                dve.sem_inc(var_ready, 1)
                dve.wait_ge(sd_ready, nth + 1)
                link(dve.reciprocal(sd, sd))
                link(dve.tensor_tensor(scale, g, sd, ALU.mult))
                link(dve.tensor_tensor(c1("mean_scale"), mv[:, 0:1], scale, ALU.mult))
                link(dve.tensor_tensor(bias, be, c1("mean_scale"), ALU.subtract))

            all_stats = stats[:, 0].rearrange("p n s -> p (n s)")
            per_chunk_stats(y1_stored, BATCH, y1_stats)
            dve.wait_ge(y1_stats, NALL)
            bn_coefs(0, all_stats, c1("g1"), c1("be1"), c1("scale1"), c1("bias1"), c1("var"),
                     c1("sd"), 0, mean_var[:, 0])
            dve.sem_inc(bn1_ready, 1)
            dve.wait_ge(setup_mm, 7)
            copy(w3_t[:, :], ps[:, 1, 0:CIN]).then_inc(dve_step, 1)
            copy(c1("gamma"), ps[:, 7, 0:1]).then_inc(dve_step, 1)
            chain[0] += 2
            for k, (_, src, hi, lo) in enumerate(setup_parts):
                dve.wait_ge(setup_hi, k + 1)
                dve.tensor_tensor(lo, src, hi.bitcast(F32), ALU.subtract).then_inc(dve_step, 1)
                chain[0] += 1
            dve.wait_ge(dve_step, chain[0])
            dve.sem_inc(setup_done, 1)
            dve.memset(zero, 0.0).then_inc(zero_made, 1)
            dve.wait_ge(pad_zeroed, 2)
            with dve.Fori(0, NCH) as j:
                for b in range(BATCH):
                    dve.wait_ge(y1_act, j * BATCH + b + 1)
                    src = y1_f[:, b].rearrange("p (r c) -> p r c", c=IMG)
                    copy(padded(y1_hi, b, j * ROWS + 1, ROWS, 1), src).then_inc(y1_hi_done, 1)
                    dve.wait_ge(y1_hi_done, j * BATCH + b + 1)
                    dve.tensor_tensor(padded(y1_lo, b, j * ROWS + 1, ROWS, 1), src,
                                      padded(y1_hi, b, j * ROWS + 1, ROWS, 1).bitcast(F32),
                                      ALU.subtract).then_inc(y1_split, 1)
            per_chunk_stats(y2_stored, BATCH, y2_stats)
            dve.wait_ge(y2_stats, NALL)
            dve.wait_ge(late_loaded, 16 * N_LATE)
            bn_coefs(0, all_stats, c1("g2"), c1("be2"), c1("scale2"), c1("bias2"), c1("var"),
                     c1("sd"), 1, mean_var[:, 0])
            dve.sem_inc(bn2_ready, 1)
            with dve.Fori(0, NCH) as j:
                for b in range(BATCH):
                    n = j * BATCH + b
                    dve.wait_ge(y2_act, n + 1)
                    dve.bn_stats(stats_at(0, n), chunk_of(b, j)).then_inc(y2_stats, 1)
            dve.wait_ge(y2_stats, 2 * NALL)
            link(dve.bn_aggr(mean_var[:, 0], all_stats))
            link(dve.tensor_scalar(c1("neg_mean2"), mean_var[:, 0, 0:1], -1.0, None, ALU.mult))
            dve.sem_inc(y2_mean, 1)
            with dve.Fori(0, NCH) as j:
                for b in range(BATCH):
                    n = j * BATCH + b
                    copy(y2_hi[:, b, bass.ds(j * CHUNK, CHUNK)], chunk_of(b, j))\
                        .then_inc(y2_hi_done, 1)
                    dve.wait_ge(y2_turned, BATCH + n + 1)
                    dve.wait_ge(gram_free, n + 1)
                    copy(y2t_slot(b), ps[0:QSUB, b, :]).then_inc(y2_t_ready, 1)
                    dve.wait_ge(y2_hi_done, n + 1)
                    dve.tensor_tensor(y2_lo[:, b, bass.ds(j * CHUNK, CHUNK)], chunk_of(b, j),
                                      y2_hi[:, b, bass.ds(j * CHUNK, CHUNK)].bitcast(F32),
                                      ALU.subtract).then_inc(y2_split, 1)
            cov, wcov, wmean = tmp[0], tmp[1], tmp[3]
            dve.wait_ge(gram_done, 1)
            link(dve.scalar_tensor_tensor(cov[:, 0:PART], ps[:, 4, 0:PART], 1.0 / TOTAL,
                                          groups[:, :], ALU.mult, ALU.mult))
            link(dve.tensor_scalar(wmean[:, :], w3_t[:, :], mean_var[:, 0, 0:1], None, ALU.mult))
            dve.sem_inc(cov_ready, 1)
            dve.wait_ge(wcov_done, 1)
            link(dve.tensor_tensor(wcov[:, :], ps[:, 5, 0:CIN], w3_t[:, :], ALU.mult))
            dve.sem_inc(cov_ready, 1)
            dve.wait_ge(wcov_done, 2)
            link(dve.tensor_scalar(tmp[1][:, :], ps[:, 6, 0:CIN], 0.0, EPS, ALU.max, ALU.add))
            dve.sem_inc(var_ready, 1)
            link(dve.tensor_tensor(tmp[4][:, :], ps[:, 7, 0:CIN], b3_b[:, :], ALU.add))
            link(dve.tensor_tensor(tmp[5][:, :], b3_b[:, :], tmp[4][:, :], ALU.subtract))
            dve.wait_ge(sd_ready, 3)
            link(dve.reciprocal(tmp[1][:, :], tmp[2][:, :]))
            link(dve.tensor_tensor(tmp[2][:, :], tmp[1][:, :], g3_b[:, :], ALU.mult))
            link(dve.tensor_tensor(tmp[3][:, :], w3_t[:, :], tmp[2][:, :], ALU.mult))
            link(copy(ws_hi[:, :], tmp[3][:, :]))
            link(dve.tensor_tensor(ws_lo[:, :], tmp[3][:, :], ws_hi[:, :].bitcast(F32),
                                   ALU.subtract))
            dve.sem_inc(ws_ready, 1)
            link(dve.tensor_tensor(tmp[4][:, :], tmp[5][:, :], tmp[2][:, :], ALU.mult))
            link(dve.tensor_tensor(tmp[5][:, :], tmp[4][:, :], be3_b[:, :], ALU.add))
            link(copy(bias_hi[:, :], tmp[5][:, :]))
            link(dve.tensor_tensor(bias_lo[:, :], tmp[5][:, :], bias_hi[:, :].bitcast(F32),
                                   ALU.subtract))
            dve.sem_inc(bias_ready, 1)
            for g in range(BLOCKS):
                link(block_weights(dve, 0, ws_hi, g))
            dve.sem_inc(path_w_ready, 1)

            by_dve = [p for p in range(PATHS) if p not in BY_ACT]

            def paths_of(j, b, previous):
                n = j * BATCH + b
                dve.wait_ge(x_again_in[b % 2], (j * 2 + b // 2 + 1) * 16)
                for k, p in enumerate(by_dve):
                    dve.wait_ge(z_done, n * PATHS + p + 1)
                    s, acc = 2 * (p % PAIRRING), dve_sum[k % 2][:, :, :]
                    z = ps[:, s:s + 2, 0:CHUNK]
                    if k < 2:
                        dve.wait_ge(dve_added, ONE + n)
                    else:
                        dve.wait_ge(dve_read, (n + 1) * N_DVE + k - 1)
                    if k == 1:
                        dve.tensor_scalar(acc, z, 0.0, None, ALU.max).then_inc(dve_read, 1)
                    else:
                        dve.scalar_tensor_tensor(
                            acc, z, 0.0, x_again[b % 2][:, :, :] if k == 0 else acc,
                            ALU.max, ALU.add).then_inc(dve_read, 1)
                    if previous and k in FINISH_AFTER:
                        finish(*previous, FINISH_AFTER.index(k))
                dve.wait_ge(dve_read, (n + 2) * N_DVE)
                dve.wait_ge(s_stored[b % 2], 16 + (j * 2 + b // 2) * 16)
                dve.tensor_tensor(s_out[b % 2][:, :, :], dve_sum[0][:, :, :],
                                  dve_sum[1][:, :, :], ALU.add).then_inc(dve_added, 1)

            def finish(j, b, step):
                n, i = j * BATCH + b, b % 2
                if step == 0:
                    dve.wait_ge(dve_added, ONE + n + 1)
                    dve.wait_ge(pool_added, ACTRING + (n + 1) * (N_ACT - 1))
                    dve.tensor_tensor(s_out[i][:, :, :], s_out[i][:, :, :],
                                      pool_sum[i][:, :, :], ALU.add).then_inc(s_ready, 1)
                else:
                    dve.wait_ge(s_ready, 2 + n + 1)
                    for k in range(HALVES):
                        dve.bn_stats(stats_at(k, n), s_out[i][:, k]).then_inc(s_stats, 1)

            paths_of(0, 0, None)
            with dve.Fori(0, NCH - 1) as j:
                for b in range(1, BATCH):
                    paths_of(j, b, (j, b - 1))
                paths_of(j + 1, 0, (j, BATCH - 1))
            for b in range(1, BATCH):
                paths_of(NCH - 1, b, (NCH - 1, b - 1))
            for step in range(2):
                finish(NCH - 1, BATCH - 1, step)
            dve.wait_ge(s_stats, NALL * HALVES)
            for k in range(HALVES):
                bn_coefs(k, stats[:, k].rearrange("p n s -> p (n s)"), c1("g4", 2)[:, k:k + 1],
                         c1("be4", 2)[:, k:k + 1], c1("scale4", 2)[:, k:k + 1],
                         c1("bias4", 2)[:, k:k + 1], c1(f"var4_{k}"), c1(f"sd4_{k}"), 3 + k,
                         mean_var[:, k])
            dve.sem_inc(bn4_ready, 1)


            def prep(g, slot):
                dve.wait_ge(xq_loaded, g * 16 + 16)
                for k in range(HALVES):
                    dve.tensor_scalar(slot(xq_f)[:, k], slot(xq_f)[:, k],
                                      c1("scale4", 2)[:, k:k + 1], c1("bias4", 2)[:, k:k + 1],
                                      ALU.mult, ALU.add).then_inc(xq_step, 1)
                dve.wait_ge(xq_step, g * 3 + 2)
                copy(slot(xq_hi), slot(xq_f)).then_inc(xq_step, 1)
                dve.wait_ge(xq_step, g * 3 + 3)
                dve.tensor_tensor(slot(xq_lo), slot(xq_f), slot(xq_hi).bitcast(F32), ALU.subtract)\
                    .then_inc(xq_split, 1)

            prep(0, lambda t: t[:, 0])
            prep(1, lambda t: t[:, 1])

            with dve.Fori(0, BATCH) as b:
                units = proj_units()
                at = 0

                def lows(q, at):
                    for u in (u for u in units if u[0] == q):
                        dve.wait_ge(proj_hi, b * UNITS + at + 1)
                        dve.tensor_tensor(u[3], ps_unit(at, u), u[2].bitcast(F32), ALU.subtract)\
                            .then_inc(proj_lo, 1)
                        at += 1
                    return at

                for q, w in enumerate(PIECES):
                    n = b * len(PIECES) + q
                    dve.wait_ge(xp_normed, n * HALVES + HALVES)
                    if q >= 2:
                        dve.wait_ge(proj_done, b * UNITS + sum(u[0] <= q - 2 for u in units))
                    i = q % 2
                    copy(xp_hi[i][:, :, 0:w], xp_f[i][:, :, 0:w]).then_inc(xp_hi_done, 1)
                    dve.wait_ge(xp_hi_done, n + 1)
                    dve.tensor_tensor(xp_lo[i][:, :, 0:w], xp_f[i][:, :, 0:w],
                                      xp_hi[i][:, :, 0:w].bitcast(F32), ALU.subtract)\
                        .then_inc(xp_split, 1)
                    if q:
                        at = lows(q - 1, at)
                lows(len(PIECES) - 1, at)

                def running_max(n, i):
                    if i == 0:
                        return
                    m = MT[i]
                    dve.wait_ge(s_evac, ONE + n * NMT + i + 1)
                    if i > 1:
                        dve.wait_ge(max_done, n * (NMT - 1) + i - 1)
                    dve.tensor_tensor(row_max[0:m, :], scores[0:m, i],
                                      scores[0:m, 0] if i == 1 else row_max[0:m, :], ALU.max)\
                        .then_inc(max_done, 1)

                def low(g, i):
                    m = MT[i]
                    dve.wait_ge(hi_done, g * NMT + i + 1)
                    dve.tensor_tensor(p_lo[0:m, i % PRING], p_f[0:m, i % PRING],
                                      p_hi[0:m, i % PRING].bitcast(F32), ALU.subtract)\
                        .then_inc(lo_done, 1)

                def spread(values, out):
                    return dve.tensor_tensor(
                        out[:, :, :],
                        ident[0:QSUB, 0:QSUB].unsqueeze(1).to_broadcast([QSUB, 4, QSUB]),
                        values[:, :].unsqueeze(2).to_broadcast([QSUB, 4, QSUB]), ALU.mult)

                def maxima(g):
                    dve.wait_ge(max_turned, g + 1)
                    dve.tensor_reduce(max_q[:, :],
                                      ps[0:QSUB, BANK_MAX, :].rearrange("p (a n) -> p a n", a=4),
                                      AX.X, ALU.max).then_inc(maxq_done, 1)
                    dve.wait_ge(maxq_done, g + 1)
                    spread(max_q, diag).then_inc(diag_done, 1)

                def inverses(g):
                    dve.wait_ge(l_done, ONE + g + 1)
                    dve.reciprocal(inv_q[:, :], ps[0:QSUB, BANK_SUM, 0:4]).then_inc(inv_step, 1)
                    dve.wait_ge(inv_step, 2 * g + 1)
                    dve.tensor_scalar(inv_q[:, :], inv_q[:, :], c1("gamma")[0:QSUB], None,
                                      ALU.mult).then_inc(inv_step, 1)
                    dve.wait_ge(inv_step, 2 * g + 2)
                    spread(inv_q, inv_diag).then_inc(inv_diag_done, 1)

                def scale_out(g):
                    dve.wait_ge(inv_spread, g + 1)
                    for k in range(HALVES):
                        dve.wait_ge(o_evac, ONE + g * HALVES + k + 1)
                        dve.tensor_tensor(o_buf[:, k], o_buf[:, k], ps[:, BANK_SUM, 0:CHUNK],
                                          ALU.mult).then_inc(o_scaled, 1)

                def stage(g, ahead, late):
                    dve.wait_ge(maxb_done, g + 1)
                    dve.wait_ge(sub_done, ONE + g * NMT)
                    copy(max_b[:, :], ps[:, BANK_MAX, 0:CHUNK]).then_inc(maxb_ready, 1)
                    dve.wait_ge(maxb_ready, ONE + g + 1)
                    for i in range(NMT + 2):
                        if i < NMT:
                            m = MT[i]
                            if i == 0 or i >= PRING:
                                k = i - PRING + 1 if i else 0
                                dve.wait_ge(lo_done, ONE + g * NMT + k)
                                dve.wait_ge(sum_added,
                                            ONE + g * (NMT - 1) + (max(1, k - 1) if i else 0))
                            dve.tensor_tensor(p_f[0:m, i % PRING], scores[0:m, i], max_b[0:m, :],
                                              ALU.subtract).then_inc(sub_done, 1)
                        if ahead and 1 <= i <= NMT:
                            running_max(g + 1, i - 1)
                        if i >= 2:
                            low(g, i - 2)
                        if i == NMT // 2:
                            prep(g + 2, lambda t: xq_slot(t, g % 2))
                        if late and i == AT_SCALE:
                            scale_out(g - 1)
                    if ahead:
                        maxima(g + 1)
                    inverses(g)

                for i in range(NMT):
                    running_max(b * NCH, i)
                maxima(b * NCH)
                stage(b * NCH, True, False)
                with dve.Fori(1, NCH - 1) as j:
                    stage(b * NCH + j, True, True)
                stage(b * NCH + NCH - 1, False, True)
                scale_out(b * NCH + NCH - 1)

        @block.tensor
        def _(pe):
            def mm(out, lhsT, rhs, start=True, stop=True):
                return nc.tensor.matmul(out, lhsT, rhs, start=start, stop=stop)

            def products(out, pairs, first=True, last=True):
                for n, (lhsT, rhs) in enumerate(pairs):
                    ins = mm(out, lhsT, rhs, start=first and n == 0,
                             stop=last and n == len(pairs) - 1)
                return ins

            for free, n in ((gram_free, 2), (pv_done, ONE), (l_done, ONE)):
                pe.sem_inc(free, n)
            pe.wait_ge(consts_made, 6)
            pe.wait_ge(w1_loaded, 2 * 16)
            for k in range(HALVES):
                ins = nc.tensor.transpose(ps[:, 7, k * PART:(k + 1) * PART],
                                          w1_n[:, k * PART:(k + 1) * PART], ident[:, :])
            ins.then_inc(w1_turned, 1)

            pe.wait_ge(w1_ready, 1)
            with pe.Fori(0, NCH) as j:
                for b in range(BATCH):
                    pe.wait_ge(x_loaded[b], j * 16 + 16)
                    pe.wait_ge(y1_stored, j * BATCH + b + 1)
                    products(ps[:, b, 0:CHUNK], [(w1_t[:, k], x_ring[:, b, k])
                                                 for k in range(HALVES)]).then_inc(conv1_done, 1)

            pe.wait_ge(weights_loaded, 16 * N_WEIGHTS)
            pe.wait_ge(y1_stored, BATCH + NALL)
            for k in range(HALVES):
                ins = nc.tensor.transpose(ps[:, 1, k * PART:(k + 1) * PART], w3_n[:, k, :],
                                          ident[:, :])
            ins.then_inc(setup_mm, 1)
            for k in range(HALVES):
                for q in range(HALVES):
                    ins = mm(ps[:, 5, k * CIN:(k + 1) * CIN], wk_n[:, q, k * PART:(k + 1) * PART],
                             wq_n[:, q, :], start=q == 0, stop=q == HALVES - 1)
            ins.then_inc(setup_mm, 1)
            for k in range(HALVES):
                for q in range(HALVES):
                    at = k * CIN + q * PART
                    ins = nc.tensor.transpose(ps[:, 6, at:at + PART],
                                              wv_n[:, q, k * PART:(k + 1) * PART], ident[:, :])
            ins.then_inc(setup_mm, 1)
            mm(ps[:, 7, 0:1], ones[0:1, :], gamma_row[:, :]).then_inc(setup_mm, 1)
            pe.wait_ge(taps_made, 1)
            for t in range(TAPS):
                ins = nc.tensor.transpose(ps[:, 2 + t // 4, (t % 4) * PART:(t % 4 + 1) * PART],
                                          taps_f[:, t, :], ident[:, :])
                if t % 4 == 3 or t == TAPS - 1:
                    ins.then_inc(setup_mm, 1)

            pe.wait_ge(setup_done, 1)
            def conv2(j, b, rows_ready):
                pe.wait_ge(y1_split, BATCH + rows_ready)
                pe.wait_ge(y2_stored, j * BATCH + b + 1)
                pairs = []
                for t in range(TAPS):
                    dy, dx = divmod(t, 3)
                    hi = padded(y1_hi, b, j * ROWS + dy, ROWS, dx)
                    lo = padded(y1_lo, b, j * ROWS + dy, ROWS, dx)
                    pairs += [(taps_hi[:, t], hi), (taps_hi[:, t], lo), (taps_lo[:, t], hi)]
                out = ps[:, b, 0:CHUNK].rearrange("p (r c) -> p r c", c=IMG)
                products(out, pairs).then_inc(conv2_done, 1)

            with pe.Fori(0, NCH - 1) as j:
                for b in range(BATCH):
                    conv2(j, b, (j + 1) * BATCH + b + 1)
            for b in range(BATCH):
                conv2(NCH - 1, b, NALL)

            gram = ps[:, 4, 0:PART]
            pe.wait_ge(zero_made, 1)
            mm(gram, zero, zero, start=True, stop=False)
            with pe.Fori(0, NCH) as j:
                def turn(b):
                    pe.wait_ge(y2_centred, j * BATCH + b + 1)
                    pe.wait_ge(y2_t_ready, j * BATCH + b + 1)
                    for q in range(4):
                        ins = nc.tensor.transpose(ps[0:QSUB, b, q * PART:(q + 1) * PART],
                                                  y2_c[:, b, q * QSUB:(q + 1) * QSUB], ident[:, :])
                    ins.then_inc(y2_turned, 1)

                def gram_of(b):
                    pe.wait_ge(y2_t_ready, BATCH + j * BATCH + b + 1)
                    for q in range(4):
                        piece = y2t_slot(b)[:, q * PART:(q + 1) * PART]
                        ins = mm(gram, piece, piece, start=False, stop=False)
                    ins.then_inc(gram_free, 1)

                turn(0)
                for b in range(1, BATCH):
                    turn(b)
                    gram_of(b - 1)
                gram_of(BATCH - 1)
            mm(gram, zero, zero, start=False, stop=True).then_inc(gram_done, 1)
            pe.wait_ge(cov_ready, 1)
            mm(ps[:, 5, 0:CIN], tmp[0][:, 0:PART], w3_t[:, :]).then_inc(wcov_done, 1)
            mm(ps[:, 7, 0:CIN], groups[:, :], tmp[3][:, :])
            pe.wait_ge(cov_ready, 2)
            mm(ps[:, 6, 0:CIN], groups[:, :], tmp[1][:, :]).then_inc(wcov_done, 1)

            pe.wait_ge(path_w_ready, 1)
            pe.wait_ge(path_w_low, PATHS // 2 + BLOCKS // 2)
            pe.wait_ge(path_rows_copied, 48)
            with pe.Fori(0, NCH) as j:
                for b in range(BATCH):
                    n = j * BATCH + b
                    pe.wait_ge(staged_in[b % 2], (j * 2 + b // 2 + 1) * 16 * 3 * BLOCKS)
                    for p in range(PATHS):
                        last = (p - PAIRRING) % PATHS
                        round_ = n if p < PAIRRING else n + 1
                        if last in BY_ACT:
                            pe.wait_ge(act_read, round_ * N_ACT + BY_ACT.index(last) + 1)
                        else:
                            done = sum(q not in BY_ACT for q in range(last + 1))
                            pe.wait_ge(dve_read, round_ * N_DVE + done)
                        s = 2 * (p % PAIRRING)
                        for k in range(HALVES):
                            ins = mm(ps[:, s + k, 0:CHUNK], path_w[:, p, k * PART:(k + 1) * PART],
                                     staged[b % 2][p // BPATHS][:, :])
                        ins.then_inc(z_done, 1)

            with pe.Fori(0, BATCH) as b:
                pe.wait_ge(s_evac, ONE + b * NCH * NMT)
                for at, u in enumerate(proj_units()):
                    q = u[0]
                    pe.wait_ge(xp_split, b * len(PIECES) + q + 1)
                    pe.wait_ge(proj_lo, b * UNITS + at + 1)
                    products(ps_unit(at, u), u[1]).then_inc(proj_done, 1)
                pe.wait_ge(proj_lo, b * UNITS + UNITS + USLACK)

                def qk(n, i):
                    if i == 0:
                        pe.wait_ge(xq_split, n + 1)
                        pe.wait_ge(s_evac, ONE + n * NMT)
                    elif i >= SRING:
                        pe.wait_ge(s_evac, ONE + n * NMT + i - SRING + 1)
                    keys = slice(MOFF[i], MOFF[i] + MT[i])
                    pairs = []
                    for k in range(HALVES):
                        xh, xl = (xq_slot(t, n % 2)[:, k] for t in (xq_hi, xq_lo))
                        pairs += [(t_hi[:, k, keys], xh), (t_hi[:, k, keys], xl),
                                  (t_lo[:, k, keys], xh)]
                    products(ps[0:MT[i], i % SRING, 0:CHUNK], pairs).then_inc(qk_done, 1)

                def pv(g, i):
                    m, r = MT[i], i % PRING
                    pe.wait_ge(lo_done, ONE + g * NMT + i + 1)
                    if i == 0:
                        pe.wait_ge(o_evac, ONE + g * HALVES)
                    for k in range(HALVES):
                        c = slice(k * PART, (k + 1) * PART)
                        ins = products(ps[:, BANK_O + k, 0:CHUNK],
                                       [(v_hi[0:m, i, c], p_hi[0:m, r]),
                                        (v_hi[0:m, i, c], p_lo[0:m, r]),
                                        (v_lo[0:m, i, c], p_hi[0:m, r])],
                                       first=i == 0, last=i == NMT - 1)
                    ins.then_inc(pv_done, 1)

                def turn_max(n):
                    pe.wait_ge(max_done, n * (NMT - 1) + NMT - 1)
                    pe.wait_ge(maxb_ready, ONE + n)
                    for q in range(4):
                        ins = nc.tensor.transpose(
                            ps[0:QSUB, BANK_MAX, q * PART:(q + 1) * PART],
                            row_max[:, q * QSUB:(q + 1) * QSUB], ident[:, :])
                    ins.then_inc(max_turned, 1)

                def spread_max(g):
                    pe.wait_ge(diag_done, g + 1)
                    mm(ps[:, BANK_MAX, 0:CHUNK], ones[0:QSUB, :],
                       diag[:, :, :].rearrange("p a n -> p (a n)")).then_inc(maxb_done, 1)

                def sum_up(g):
                    pe.wait_ge(sum_added, ONE + g * (NMT - 1) + NMT - 1)
                    pe.wait_ge(out_added, ONE + g)
                    for q in range(4):
                        ins = mm(ps[0:QSUB, BANK_SUM, q:q + 1],
                                 p_sum[:, q * QSUB:(q + 1) * QSUB], ones[:, 0:1])
                    ins.then_inc(l_done, 1)

                def spread_inverses(g):
                    pe.wait_ge(inv_diag_done, g + 1)
                    mm(ps[:, BANK_SUM, 0:CHUNK], ones[0:QSUB, :],
                       inv_diag[:, :, :].rearrange("p a n -> p (a n)")).then_inc(inv_spread, 1)

                def stage(g, ahead, late):
                    spread_max(g)
                    for i in range(NMT + LAG):
                        if ahead and i < NMT:
                            qk(g + 1, i)
                        if ahead and i == NMT + LAG - 1:
                            turn_max(g + 1)
                        if i >= LAG:
                            pv(g, i - LAG)
                        if late and i == AT_SPREAD:
                            spread_inverses(g - 1)
                    sum_up(g)

                for i in range(NMT):
                    qk(b * NCH, i)
                turn_max(b * NCH)
                stage(b * NCH, True, False)
                with pe.Fori(1, NCH - 1) as j:
                    stage(b * NCH + j, True, True)
                stage(b * NCH + NCH - 1, False, True)
                spread_inverses(b * NCH + NCH - 1)


_INS = ["x", "L0_conv_w1", "L0_conv_b1", "L0_conv_g1", "L0_conv_be1", "L0_conv_w2", "L0_conv_b2",
        "L0_conv_g2", "L0_conv_be2", "L0_conv_w3", "L0_conv_b3", "L0_conv_g3", "L0_conv_be3",
        "L0_conv_g4", "L0_conv_be4", "L1_conv_Wq", "L1_conv_Wk", "L1_conv_Wv", "L1_conv_gamma"]


def kernel(**inputs):
    import numpy as np
    import concourse.bacc as bacc
    from concourse.bass_utils import run_bass_kernel_spmd

    nc = bacc.Bacc("TRN2", target_bir_lowering=False, num_devices=1)
    arrays, args = {}, []
    for name in _INS:
        a = np.ascontiguousarray(inputs[name])
        arrays[f"in_{name}"] = a
        args.append(nc.dram_tensor(f"in_{name}", a.shape, mybir.dt.from_np(a.dtype),
                                   kind="ExternalInput").ap())
    out = nc.dram_tensor("out", inputs["x"].shape, F32, kind="ExternalOutput").ap()
    conv_attention_kernel(nc, *args, out)
    return run_bass_kernel_spmd(nc, [arrays], core_ids=[0]).results[0]["out"]
```
